# Optimizing a Trainium2 kernel written in Bass

```python
import numpy as np
import jax
import jax.numpy as jnp

def _softmax(x, axis=-1):
    return jax.nn.softmax(x, axis=axis)

def _gelu(x):
    return jax.nn.gelu(x, approximate=True)

def _silu(x):
    return jax.nn.silu(x)

def _sigmoid(x):
    return jax.nn.sigmoid(x)

def _layernorm(x, axis=-1, eps=1e-05):
    m = jnp.mean(x, axis=axis, keepdims=True)
    v = jnp.var(x, axis=axis, keepdims=True)
    return (x - m) / jnp.sqrt(v + eps)

def _scatter_add(tgt, idx, src, axis=0):
    return tgt.at[idx].add(src)

def _segment_sum(src, seg, n):
    return jax.ops.segment_sum(src, seg, n)
kernel_name = 'mk_gps_d1_gnn_r32_cba17b'

def setup_inputs(seed: int=0):
    np.random.seed(seed)
    _w = jnp.asarray

    def _rec_inputs():
        import jax
        import jax.numpy as jnp
        _gk = jax.random.key(seed)
        x = -8.776e-05 + 1 * jax.random.normal(jax.random.fold_in(_gk, 1), (625, 256), jnp.float32)
        _s = jax.random.randint(jax.random.fold_in(_gk, 2), (10000,), 0, 625, jnp.int32)
        _d = jax.random.randint(jax.random.fold_in(_gk, 3), (10000,), 0, 625, jnp.int32)
        _loop = jnp.arange(625, dtype=jnp.int32)
        src = jnp.concatenate([_s, _d, _loop])
        dst = jnp.concatenate([_d, _s, _loop])
        _o = jnp.argsort(dst, stable=True)
        src = src[_o]
        dst = dst[_o]
        edge_weight = jax.random.uniform(jax.random.fold_in(_gk, 12), (20625,), jnp.float32, 0.0, 0.999998)
        return (x, src, dst, edge_weight)
    x, src, dst, edge_weight = _rec_inputs()

    def _L0_gnn_setup():
        import jax, jax.numpy as jnp
        import numpy as np
        N = 625
        E = 10000
        D_IN = 256
        D_OUT = 256
        BN_EPS = 1e-05

        def _batchnorm(h, gamma, beta):
            mean = jnp.mean(h, axis=0)
            var = jnp.var(h, axis=0)
            return (h - mean) * jax.lax.rsqrt(var + BN_EPS) * gamma + beta
        key = jax.random.key(seed)
        ks = jax.random.split(key, 10)
        x = jax.random.normal(ks[0], (N, D_IN), dtype=jnp.float32)
        edge_index = jax.random.randint(ks[1], (2, E), 0, N, dtype=jnp.int64)
        edge_weight = jax.random.uniform(ks[2], (E,), dtype=jnp.float32)
        s1 = 1.0 / np.sqrt(D_IN)
        s2 = 1.0 / np.sqrt(D_OUT)
        W1 = jax.random.uniform(ks[3], (D_IN, D_OUT), minval=-s1, maxval=s1, dtype=jnp.float32)
        b1 = jax.random.uniform(ks[4], (D_OUT,), minval=-s1, maxval=s1, dtype=jnp.float32)
        g1 = jnp.ones((D_OUT,), jnp.float32)
        be1 = jnp.zeros((D_OUT,), jnp.float32)
        W2 = jax.random.uniform(ks[5], (D_OUT, D_OUT), minval=-s2, maxval=s2, dtype=jnp.float32)
        b2 = jax.random.uniform(ks[6], (D_OUT,), minval=-s2, maxval=s2, dtype=jnp.float32)
        g2 = jnp.ones((D_OUT,), jnp.float32)
        be2 = jnp.zeros((D_OUT,), jnp.float32)
        eps = jnp.zeros((1,), jnp.float32)
        return {'x': x, 'edge_index': edge_index, 'edge_weight': edge_weight, 'W1': W1, 'b1': b1, 'g1': g1, 'be1': be1, 'W2': W2, 'b2': b2, 'g2': g2, 'be2': be2, 'eps': eps}
    _L0_gnn_all = _L0_gnn_setup()
    _L0_gnn_in = {k: v for k, v in _L0_gnn_all.items() if k in ('W1', 'b1', 'g1', 'be1', 'W2', 'b2', 'g2', 'be2', 'eps')}
    del _L0_gnn_all

    def _L0_mix_setup():
        import jax, jax.numpy as jnp
        import numpy as np
        A, Bc, Cc = (0.5, 1.0, 1.0)
        H = 8
        EPS = 1e-12

        def _normalize(t):
            n = jnp.linalg.norm(t, axis=-1, keepdims=True)
            return t / jnp.maximum(n, EPS)
        key = jax.random.key(seed)
        ks = jax.random.split(key, 5)
        B, N, C = (8, 64, 256)
        D = C // H
        x = jax.random.normal(ks[0], (B, N, C), dtype=jnp.float32)
        Wqkv = jax.random.normal(ks[1], (3 * H * D, C), dtype=jnp.float32) * 0.02
        bqkv = jnp.zeros((3 * H * D,), dtype=jnp.float32)
        Wproj = jax.random.normal(ks[2], (C, H * D), dtype=jnp.float32) * 0.02
        bproj = jnp.zeros((C,), dtype=jnp.float32)
        temperature = jnp.ones((1, H, 1, 1), dtype=jnp.float32)
        return {'x': x, 'Wqkv': Wqkv, 'bqkv': bqkv, 'Wproj': Wproj, 'bproj': bproj, 'temperature': temperature}
    _L0_mix_all = _L0_mix_setup()
    _L0_mix_in = {k: v for k, v in _L0_mix_all.items() if k in ('Wqkv', 'bqkv', 'Wproj', 'bproj', 'temperature')}
    del _L0_mix_all

    def _L0_ffn_setup():
        import jax, jax.numpy as jnp
        import numpy as np
        B, T, D, H, E = (16, 128, 256, 512, 8)
        key = jax.random.key(seed)
        ks = jax.random.split(key, 5)
        x = jax.random.normal(ks[0], (B, T, D), dtype=jnp.float32)
        gate_w = jax.random.normal(ks[1], (D, E), dtype=jnp.float32) * 0.02
        gate_b = jnp.zeros((E,), dtype=jnp.float32)
        W1 = jax.random.normal(ks[2], (E, D, H), dtype=jnp.float32) * 0.02
        b1 = jnp.zeros((E, H), dtype=jnp.float32)
        W2 = jax.random.normal(ks[3], (E, H, D), dtype=jnp.float32) * 0.02
        b2 = jnp.zeros((E, D), dtype=jnp.float32)
        return {'x': x, 'gate_w': gate_w, 'gate_b': gate_b, 'W1': W1, 'b1': b1, 'W2': W2, 'b2': b2}
    _L0_ffn_all = _L0_ffn_setup()
    _L0_ffn_in = {k: v for k, v in _L0_ffn_all.items() if k in ('gate_w', 'gate_b', 'W1', 'b1', 'W2', 'b2')}
    del _L0_ffn_all
    return {'x': x, 'src': src, 'dst': dst, 'edge_weight': edge_weight, 'L0_gnn_W1': _L0_gnn_in['W1'], 'L0_gnn_b1': _L0_gnn_in['b1'], 'L0_gnn_g1': _L0_gnn_in['g1'], 'L0_gnn_be1': _L0_gnn_in['be1'], 'L0_gnn_W2': _L0_gnn_in['W2'], 'L0_gnn_b2': _L0_gnn_in['b2'], 'L0_gnn_g2': _L0_gnn_in['g2'], 'L0_gnn_be2': _L0_gnn_in['be2'], 'L0_gnn_eps': _L0_gnn_in['eps'], 'L0_mix_Wqkv': _L0_mix_in['Wqkv'], 'L0_mix_bqkv': _L0_mix_in['bqkv'], 'L0_mix_Wproj': _L0_mix_in['Wproj'], 'L0_mix_bproj': _L0_mix_in['bproj'], 'L0_mix_temperature': _L0_mix_in['temperature'], 'L0_ffn_gate_w': _L0_ffn_in['gate_w'], 'L0_ffn_gate_b': _L0_ffn_in['gate_b'], 'L0_ffn_W1': _L0_ffn_in['W1'], 'L0_ffn_b1': _L0_ffn_in['b1'], 'L0_ffn_W2': _L0_ffn_in['W2'], 'L0_ffn_b2': _L0_ffn_in['b2']}

def reference(x, src, dst, edge_weight, L0_gnn_W1, L0_gnn_b1, L0_gnn_g1, L0_gnn_be1, L0_gnn_W2, L0_gnn_b2, L0_gnn_g2, L0_gnn_be2, L0_gnn_eps, L0_mix_Wqkv, L0_mix_bqkv, L0_mix_Wproj, L0_mix_bproj, L0_mix_temperature, L0_ffn_gate_w, L0_ffn_gate_b, L0_ffn_W1, L0_ffn_b1, L0_ffn_W2, L0_ffn_b2):
    import jax
    import jax.numpy as jnp

    def _L0_gnn_ref(x, edge_index, edge_weight, W1, b1, g1, be1, W2, b2, g2, be2, eps):
        import jax, jax.numpy as jnp
        import numpy as np
        N = 625
        E = 10000
        D_IN = 256
        D_OUT = 256
        BN_EPS = 1e-05

        def _batchnorm(h, gamma, beta):
            mean = jnp.mean(h, axis=0)
            var = jnp.var(h, axis=0)
            return (h - mean) * jax.lax.rsqrt(var + BN_EPS) * gamma + beta
        src = edge_index[0]
        dst = edge_index[1]
        msg = edge_weight[:, None] * x[src]
        agg = jax.ops.segment_sum(msg, dst, num_segments=N)
        out = agg + (1.0 + eps[0]) * x
        h = out @ W1 + b1
        h = _batchnorm(h, g1, be1)
        h = h @ W2 + b2
        h = _batchnorm(h, g2, be2)
        return h

    def _L0_mix_ref(x, Wqkv, bqkv, Wproj, bproj, temperature):
        import jax, jax.numpy as jnp
        import numpy as np
        A, Bc, Cc = (0.5, 1.0, 1.0)
        H = 8
        EPS = 1e-12

        def _normalize(t):
            n = jnp.linalg.norm(t, axis=-1, keepdims=True)
            return t / jnp.maximum(n, EPS)
        B, N, C = x.shape
        D = C // H
        scale = float(D) ** 0.25
        qkv = (x @ Wqkv.T + bqkv).reshape(B, N, 3, H, D)
        qkv = jnp.transpose(qkv, (2, 0, 3, 1, 4))
        q, k, v = (qkv[0], qkv[1], qkv[2])
        q = q * scale
        v1 = jnp.concatenate([jnp.ones((B, H, N, 1), dtype=v.dtype), v], axis=-1)
        qn = _normalize(q) * (scale * temperature)
        kn = _normalize(k) * scale
        vN = v1 / N
        kv_mod = jnp.einsum('bhni,bhnj,bhne->bhije', kn, kn, vN)
        kv = jnp.einsum('bhnd,bhne->bhde', kn, vN)
        vsum = jnp.sum(vN, axis=-2)[:, :, None, :]
        y = A * jnp.einsum('bhni,bhnj,bhije->bhne', qn, qn, kv_mod) + scale ** 2 * Bc * jnp.einsum('bhnd,bhde->bhne', qn, kv) + scale ** 4 * Cc * vsum
        y_norm, y = (y[..., :1], y[..., 1:])
        y = y / y_norm
        out = jnp.transpose(y, (0, 2, 1, 3)).reshape(B, N, H * D)
        return out @ Wproj.T + bproj

    def _L0_ffn_ref(x, gate_w, gate_b, W1, b1, W2, b2):
        import jax, jax.numpy as jnp
        import numpy as np
        B, T, D, H, E = (16, 128, 256, 512, 8)
        Bb, Tt, Dd = x.shape
        Ee = gate_w.shape[1]
        xf = x.reshape(-1, Dd)
        N = xf.shape[0]
        logits = xf @ gate_w + gate_b
        probs = jax.nn.softmax(logits, axis=-1)
        top2_vals, top2_idx = jax.lax.top_k(probs, 2)
        cw = jnp.zeros((N, Ee), dtype=xf.dtype).at[jnp.arange(N)[:, None], top2_idx].add(top2_vals)

        def step(acc, params):
            w1, bb1, w2, bb2, we = params
            h = jax.nn.gelu(xf @ w1 + bb1, approximate=False)
            y = h @ w2 + bb2
            return (acc + we[:, None] * y, None)
        out, _ = jax.lax.scan(step, jnp.zeros_like(xf), (W1, b1, W2, b2, cw.T))
        return out.reshape(Bb, Tt, Dd)
    edge_index = jnp.stack([src, dst])
    xn = _layernorm(x, axis=-1)
    x = x + _L0_gnn_ref(xn, edge_index, edge_weight, L0_gnn_W1, L0_gnn_b1, L0_gnn_g1, L0_gnn_be1, L0_gnn_W2, L0_gnn_b2, L0_gnn_g2, L0_gnn_be2, L0_gnn_eps) + _L0_mix_ref(xn[None], L0_mix_Wqkv, L0_mix_bqkv, L0_mix_Wproj, L0_mix_bproj, L0_mix_temperature)[0]
    x = x + _L0_ffn_ref(_layernorm(x, axis=-1)[None], L0_ffn_gate_w, L0_ffn_gate_b, L0_ffn_W1, L0_ffn_b1, L0_ffn_W2, L0_ffn_b2)[0]
    return x

_drawn_inputs = setup_inputs


def setup_inputs(seed=0):
    import zlib

    import numpy as np

    out = dict(_drawn_inputs(seed))
    spreads = {'L0_gnn_g1': (1.0, 0.2),
     'L0_gnn_be1': (0.0, 0.8),
     'L0_gnn_g2': (1.0, 0.2),
     'L0_gnn_be2': (0.0, 0.1),
     'L0_mix_bqkv': (0.0, 0.387),
     'L0_mix_bproj': (0.0, 0.1),
     'L0_mix_temperature': (1.0, 0.6),
     'L0_ffn_gate_b': (0.0, 0.62),
     'L0_ffn_b1': (0.0, 0.8),
     'L0_ffn_b2': (0.0, 0.452)}
    factors = {'L0_gnn_b1': 8.0,
     'L0_gnn_b2': 8.0,
     'L0_mix_Wqkv': 8.0,
     'L0_mix_Wproj': 2.706,
     'L0_ffn_gate_w': 2.803,
     'L0_ffn_W1': 4.149,
     'L0_ffn_W2': 3.916}
    for name, (base, spread) in spreads.items():
        noise = np.random.default_rng([zlib.crc32(name.encode()), seed]).standard_normal(out[name].shape)
        drawn = base * np.exp(spread * noise) if base else spread * noise
        out[name] = jnp.asarray(drawn.astype(out[name].dtype))
    for name, factor in factors.items():
        out[name] = (out[name] * factor).astype(out[name].dtype)
    return out
```

```python
from contextlib import ExitStack

import concourse.bass as bass
from concourse import mybir

F32 = mybir.dt.float32
BF16 = mybir.dt.bfloat16
I32 = mybir.dt.int32
ALU = mybir.AluOpType
ACT = mybir.ActivationFunctionType
AX = mybir.AxisListType
RMAX = bass.bass_isa.ReduceOp.max

N = 625
C = 256
NT, R = 5, 125
KC = C // 128
HALF = 313
NP = 2 * HALF
E = 20625
H, D = 8, 32
NX, HID = 8, 512
MC = HID // 128
LN_EPS = 1e-5

TILES_REG = 21
REGIONS = 8
TILES = TILES_REG * REGIONS
REAL_TILES = -(-E // 128)
STEP = 81
WIN = 18
BEFORE = 6
KEYS = WIN * NT
SLOTS = 6
TILE_OFF = [(j * 128 * N) // E for j in range(TILES_REG)]
REG_NODES = TILE_OFF[-1] + WIN
REG_COLS = REG_NODES * NT
AW = STEP * (REGIONS - 1) + REG_NODES

COL = {n: i for i, n in enumerate(["gb1", "gb1_", "gg1", "gg1_", "gbe1", "gbe1_",
                                   "gb2", "gb2_", "gg2", "gg2_", "gbe2", "gbe2_"])}
COL_FB1 = 12
COLS = COL_FB1 + NX * MC
ROW_BQKV, ROW_BPROJ, ROW_GB, ROW_TEMP, ROW_EPS = 0, 768, 1024, 1032, 1040
ROWS = 1041
CST_ID, CST_IOTA, CST_KEY = 0, 128, 256
CST_RANK = CST_KEY + TILES
CST_DST = CST_RANK + NX
CSTS = CST_DST + N

SCALE2 = float(D) ** 0.5
SCALE = float(D) ** 0.25
SHIFT = SCALE2
REST = 2.0 * (float(D) - 0.5 * SCALE2 * SCALE2)


def graph_layer(nc, x, esrc, edst, ew, cst, cols, rows, wqkvT, wprojT, gw1, gw2, gatew, fw1, fw2, fb2, out):
    with ExitStack() as ctx:
        def sb(name, shape, dt=F32):
            return ctx.enter_context(nc.sbuf_tensor(name, shape, dt))

        def sem(name):
            return ctx.enter_context(nc.semaphore(name))

        ps = ctx.enter_context(nc.psum_tensor("ps", [128, 8, 512], F32))

        x_sb = sb("x_sb", [R, NT, C])
        cst_sb = sb("cst_sb", [128, CSTS])
        cols_sb = sb("cols_sb", [128, COLS])
        rows_sb = sb("rows_sb", [128, ROWS])
        src_i = sb("src_i", [128, TILES], I32)
        dst_i = sb("dst_i", [128, TILES], I32)
        w_sb = sb("w_sb", [128, TILES])
        wqkv_sb = sb("wqkv_sb", [128, KC, 3 * C])
        wproj_sb = sb("wproj_sb", [128, KC, C])
        gw1_sb = sb("gw1_sb", [128, KC, C])
        gw2_sb = sb("gw2_sb", [128, KC, C])
        gatew_sb = sb("gatew_sb", [128, KC, NX])
        fb2_sb = sb("fb2_sb", [NX, C])
        fw1_sb = sb("fw1_sb", [128, 2, KC, HID])
        fw2_sb = sb("fw2_sb", [128, 2, MC, C])
        ident = cst_sb[:, CST_ID:CST_ID + 128]
        iota = cst_sb[:, CST_IOTA:CST_IOTA + 128]

        stats = sb("stats", [128, NT, 6])
        mv = sb("mv", [128, NT, 2])
        std = sb("std", [128, NT])
        rstd = sb("rstd", [128, NT])
        xn = sb("xn", [R, NT, C])
        xnT = sb("xnT", [128, KC, NP])
        eps_c = sb("eps_c", [128, 1])
        shift_c = sb("shift_c", [128, 1])
        ones = sb("ones", [128, 32])
        rest_c = sb("rest_c", [128, 1])
        zeros = sb("zeros", [128, 512], BF16)

        srcf = sb("srcf", [128, TILES])
        dstf = sb("dstf", [128, TILES])
        chunk = sb("chunk", [128, TILES])
        srow = sb("srow", [128, TILES])
        key = sb("key", [128, TILES])
        out_lo = sb("out_lo", [128, TILES])
        out_win = sb("out_win", [128, TILES])
        w_out = sb("w_out", [128, TILES])
        any_p = sb("any_p", [128, 1])
        any_all = sb("any_all", [128, 1])
        flag = sb("flag", [128, 1], I32)
        oh_src = sb("oh_src", [128, SLOTS, R])
        oh_dst = sb("oh_dst", [128, SLOTS, KEYS])
        A = sb("A", [R, NT, AW])
        full_dst = sb("full_dst", [128, NP])
        full_src = sb("full_src", [128, R])
        in_chunk = sb("in_chunk", [128, TILES])

        qkv = sb("qkv", [R, NT, 3 * C])
        sq = sb("sq", [R, NT, 2 * C])
        ss = sb("ss", [R, NT, 2 * H])
        nrm = sb("nrm", [R, NT, 2 * H])
        qT = sb("qT", [128, KC, NP])
        kT = sb("kT", [128, KC, N])
        temp2 = sb("temp2", [R, H])
        P = sb("P", [R, 2, 4, HALF])
        vrest = sb("vrest", [128, KC])
        rden = sb("rden", [128, HALF])
        yT = sb("yT", [128, KC, NP])

        eps1 = sb("eps1", [128, 1])
        gT = sb("gT", [128, KC, NP])
        hT = sb("hT", [128, KC, NP])
        bst = sb("bst", [128, KC, 2, 6])
        bmv = sb("bmv", [128, KC, 2])
        bstd = sb("bstd", [128, KC])
        bscale = sb("bscale", [128, KC])
        bshift = sb("bshift", [128, KC])
        btmp = sb("btmp", [128, KC])
        uT = sb("uT", [128, KC, NP])

        acc = sb("acc", [R, NT, C])
        x2n = sb("x2n", [R, NT, C])
        x2T = sb("x2T", [128, KC, NP])
        prob = sb("prob", [R, NT, NX])
        red = sb("red", [R, NT])
        rank1 = sb("rank1", [R, NT, NX])
        top1 = sb("top1", [R, NT, NX])
        rest = sb("rest", [R, NT, NX])
        top2 = sb("top2", [R, NT, NX])
        cw = sb("cw", [R, NT, NX])
        cwe = sb("cwe", [R, NX, NT])
        cwT = sb("cwT", [NX, N])
        act_h = sb("act_h", [128, 2, MC, NP])

        cst_in, rows_in, cols_in, edges_in = (sem(n) for n in ("cst_in", "rows_in", "cols_in", "edges_in"))
        x_in = [sem(f"x_in{t}") for t in range(NT)]
        wqkv_in, wsmall_in = sem("wqkv_in"), sem("wsmall_in")
        fw_in = [sem("fw_in0"), sem("fw_in1")]
        out_done = sem("out_done")
        consts_set = sem("consts_set")
        dve_step = sem("dve_step")
        ln_var, ln_std, xn_ready = sem("ln_var"), sem("ln_std"), sem("xn_ready")
        xT_ps, xT_ready = sem("xT_ps"), sem("xT_ready")
        qkv_ps, qkv_ready = sem("qkv_ps"), sem("qkv_ready")
        ss_ready, nrm_ready, qk_normed = sem("ss_ready"), sem("nrm_ready"), sem("qk_normed")
        qkT_ps, qkT_ready = sem("qkT_ps"), sem("qkT_ready")
        vsum_ps, vrest_ready = sem("vsum_ps"), sem("vrest_ready")
        edges_ready, any_ready, flag_max, flag_ready = (sem(n) for n in ("edges_ready", "any_ready", "flag_max", "flag_ready"))
        slot_free, src_ready, dst_ready = sem("slot_free"), sem("src_ready"), sem("dst_ready")
        region_ps, region_added = sem("region_ps"), sem("region_added")
        full_ready, full_used, full_ps, full_added = (sem(n) for n in ("full_ready", "full_used", "full_ps", "full_added"))
        adj_zeroed, adj_ready, chunk_set = sem("adj_zeroed"), sem("adj_ready"), sem("chunk_set")
        scores_ready, squares_ready, pv_done, y_ready = (
            sem(n) for n in ("scores_ready", "squares_ready", "pv_done", "y_ready"))
        agg_ps, agg_ready = sem("agg_ps"), sem("agg_ready")
        lin_ps, lin_ready, bvar_ready, bstd_ready, bn_ready = (
            sem(n) for n in ("lin_ps", "lin_ready", "bvar_ready", "bstd_ready", "bn_ready"))
        mix_ps, mix_added = sem("mix_ps"), sem("mix_added")
        x2n_ready, x2T_ps, x2T_ready = sem("x2n_ready"), sem("x2T_ps"), sem("x2T_ready")
        gate_ps, logits_ready, exp_ready, cw_ready = sem("gate_ps"), sem("logits_ready"), sem("exp_ready"), sem("cw_ready")
        cwT_ps, cwT_ready, bias_ps = sem("cwT_ps"), sem("cwT_ready"), sem("bias_ps")
        up_ps, gelu_ready, down_ps, down_added = sem("up_ps"), sem("gelu_ready"), sem("down_ps"), sem("down_added")

        block = ctx.enter_context(nc.Block())

        UNITS = 4 * NT

        @block.sync
        def _(sp):
            for t in range(NT):
                sp.dma_start(x_sb[:, t, :], x[t * R:(t + 1) * R, :]).then_inc(x_in[t], 16)
            sp.dma_start(src_i[:, :], esrc[:, :]).then_inc(edges_in, 16)
            sp.dma_start(dst_i[:, :], edst[:, :]).then_inc(edges_in, 16)
            sp.dma_start(w_sb[:, :], ew[:, :]).then_inc(edges_in, 16)
            sp.dma_start(wqkv_sb[:, :, :], wqkvT.rearrange("(k p) n -> p k n", p=128)).then_inc(wqkv_in, 16)
            sp.dma_start(cols_sb[:, :], cols[:, :]).then_inc(cols_in, 16)
            for dst, src in ((wproj_sb, wprojT), (gw1_sb, gw1), (gw2_sb, gw2), (gatew_sb, gatew)):
                sp.dma_start(dst[:, :, :], src.rearrange("(k p) n -> p k n", p=128)).then_inc(wsmall_in, 16)
            sp.dma_start(fb2_sb[:, :], fb2[:, :]).then_inc(wsmall_in, 16)
            for s in range(2):
                sp.dma_start(fw1_sb[:, s], fw1[s].rearrange("(k p) n -> p k n", p=128)).then_inc(fw_in[s], 16)
                sp.dma_start(fw2_sb[:, s], fw2[s].rearrange("(k p) n -> p k n", p=128)).then_inc(fw_in[s], 16)
            with sp.Fori(0, NX // 2 - 1) as i:
                for s in range(2):
                    sp.wait_ge(down_ps, (i * 2 + s + 1) * NT)
                    w1 = fw1[bass.ds(i * 2 + 2 + s, 1)].rearrange("e (k p) n -> p (e k) n", p=128)
                    w2 = fw2[bass.ds(i * 2 + 2 + s, 1)].rearrange("e (k p) n -> p (e k) n", p=128)
                    sp.dma_start(fw1_sb[:, s], w1).then_inc(fw_in[s], 16)
                    sp.dma_start(fw2_sb[:, s], w2).then_inc(fw_in[s], 16)
            for t in range(NT):
                sp.wait_ge(down_added, NX * NT + t + 1)
                sp.dma_start(out[t * R:(t + 1) * R, :], acc[:, t, :]).then_inc(out_done, 16)
            sp.wait_ge(out_done, 16 * NT)

        @block.gpsimd
        def _(pool):
            nc.gpsimd.memset(A[:, :, :], 0.0).then_inc(adj_zeroed, 1)
            pool.wait_ge(any_ready, 1)
            nc.gpsimd.partition_all_reduce(any_all[:, :], any_p[:, :], 128, RMAX).then_inc(flag_max, 1)

        @block.scalar
        def _(act):
            act.dma_start(cst_sb[:, :], cst[:, :]).then_inc(cst_in, 16)
            act.dma_start(rows_sb[:, :], rows.partition_broadcast(128)).then_inc(rows_in, 16)

            act.wait_ge(consts_set, 8)
            act.wait_ge(ln_var, 1)
            nc.scalar.activation(std[0:R, :], mv[0:R, :, 1], ACT.Sqrt, bias=eps_c[0:R, :]).then_inc(ln_std, 1)

            for t in range(NT):
                act.wait_ge(xT_ps, t + 1)
                nc.scalar.copy(xnT[:, :, t * R:(t + 1) * R],
                               ps[:, 2 + t % 2, 0:KC * R].rearrange("p (m r) -> p m r", m=KC)).then_inc(xT_ready, 1)

            act.wait_ge(ss_ready, 1)
            nc.scalar.activation(nrm[:, :, 0:H], ss[:, :, 0:H], ACT.Sqrt, scale=SCALE2).then_inc(nrm_ready, 1)
            nc.scalar.activation(nrm[:, :, H:2 * H], ss[:, :, H:2 * H], ACT.Sqrt).then_inc(nrm_ready, 1)

            for t in range(NT):
                act.wait_ge(qkT_ps, t + 1)
                bank = ps[:, 2 + t % 2, 0:4 * R].rearrange("p (a m r) -> p a m r", a=2, m=KC)
                nc.scalar.copy(qT[:, :, t * R:(t + 1) * R], bank[:, 0]).then_inc(qkT_ready, 1)
                nc.scalar.copy(kT[:, :, t * R:(t + 1) * R], bank[:, 1]).then_inc(qkT_ready, 1)

            def square(u):
                for pair in range(2):
                    act.wait_ge(scores_ready, 2 * u + pair + 1)
                    if u >= 2:
                        act.wait_ge(pv_done, u - 1)
                    nc.scalar.activation(P[:, u % 2, 2 * pair:2 * pair + 2, :],
                                         ps[0:R, 4 + 2 * pair:6 + 2 * pair, 0:HALF], ACT.Square,
                                         bias=shift_c[0:R, :]).then_inc(squares_ready, 1)

            def linear_out(layer):
                for m in range(KC):
                    act.wait_ge(lin_ps, layer * KC + m + 1)
                    if layer == 1 and m == 0:
                        act.wait_ge(bn_ready, 1)
                    b = cols_sb[:, (COL["gb1"] if layer == 0 else COL["gb2"]) + m:][:, 0:1]
                    nc.scalar.activation(hT[:, m, :].rearrange("p (a n) -> p a n", a=2), ps[:, 0:2, 0:HALF],
                                         ACT.Identity, bias=b).then_inc(lin_ready, 1)

            def bn_std(layer):
                act.wait_ge(bvar_ready, layer + 1)
                nc.scalar.activation(bstd[:, :], bmv[:, :, 1], ACT.Sqrt, bias=eps_c[:, :]).then_inc(bstd_ready, 1)

            act.wait_ge(cols_in, 16)
            for u in range(UNITS):
                square(u)
                if u == 4:
                    linear_out(0)
                    bn_std(0)
                if u == 9:
                    linear_out(1)
                    bn_std(1)

            act.wait_ge(ln_var, 2)
            nc.scalar.activation(std[0:R, :], mv[0:R, :, 1], ACT.Sqrt, bias=eps_c[0:R, :]).then_inc(ln_std, 1)
            for t in range(NT):
                act.wait_ge(x2T_ps, t + 1)
                nc.scalar.copy(x2T[:, :, t * R:(t + 1) * R],
                               ps[:, t % 2, 0:KC * R].rearrange("p (m r) -> p m r", m=KC)).then_inc(x2T_ready, 1)

            act.wait_ge(logits_ready, 1)
            nc.scalar.activation(prob[:, :, :], prob[:, :, :], ACT.Exp).then_inc(exp_ready, 1)

            with act.Fori(0, NX // 2) as i:
                for s in range(2):
                    for m in range(MC):
                        g = s * MC + m
                        act.wait_ge(up_ps, i * (2 * MC) + g + 1)
                        b = cols_sb[:, bass.ds(i * (2 * MC) + (COL_FB1 + g), 1)]
                        nc.scalar.activation(act_h[:, s, m, :].rearrange("p (a n) -> p a n", a=2),
                                             ps[:, 2 * (m % 2):2 * (m % 2) + 2, 0:HALF],
                                             ACT.Gelu, bias=b).then_inc(gelu_ready, 1)

        @block.vector
        def _(dve):
            steps = [0]

            def then(ins):
                steps[0] += 1
                ins.then_inc(dve_step, 1)
                dve.wait_ge(dve_step, steps[0])

            nc.vector.memset(eps_c[:, :], LN_EPS).then_inc(consts_set, 1)
            nc.vector.memset(zeros[:, :], 0.0).then_inc(consts_set, 1)
            nc.vector.memset(shift_c[:, :], SHIFT).then_inc(consts_set, 1)
            nc.vector.memset(ones[:, :], 1.0).then_inc(consts_set, 1)
            nc.vector.memset(rest_c[:, :], REST).then_inc(consts_set, 1)
            for buf in (xnT, qT, x2T):
                nc.vector.memset(buf[:, :, N:NP], 0.0).then_inc(consts_set, 1)
            dve.wait_ge(consts_set, 8)

            def row_norm(src, dst, ready, layer):
                for t in range(NT):
                    if layer == 0:
                        dve.wait_ge(x_in[t], 16)
                    last = nc.vector.bn_stats(stats[0:R, t, :], src[:, t, :])
                then(last)
                for t in range(NT):
                    last = nc.vector.bn_aggr(mv[0:R, t, :], stats[0:R, t, :])
                last.then_inc(ln_var, 1)
                dve.wait_ge(ln_std, layer + 1)
                then(nc.vector.reciprocal(rstd[0:R, :], std[0:R, :]))
                for t in range(NT):
                    nc.vector.tensor_scalar(dst[:, t, :], src[:, t, :], mv[0:R, t, 0:1], rstd[0:R, t:t + 1],
                                            ALU.subtract, ALU.mult).then_inc(ready, 1)

            row_norm(x_sb, xn, xn_ready, 0)

            dve.wait_ge(edges_in, 48)
            dve.wait_ge(cst_in, 16)
            nc.vector.tensor_copy(srcf[:, :], src_i[:, :])
            then(nc.vector.tensor_copy(dstf[:, :], dst_i[:, :]))
            then(nc.vector.tensor_scalar(chunk[:, :], srcf[:, :], float(R), None, ALU.is_ge))
            for c in range(2, NT):
                then(nc.vector.scalar_tensor_tensor(chunk[:, :], srcf[:, :], float(c * R), chunk[:, :],
                                                    ALU.is_ge, ALU.add))
            nc.vector.scalar_tensor_tensor(srow[:, :], chunk[:, :], -float(R), srcf[:, :], ALU.mult, ALU.add)
            then(nc.vector.scalar_tensor_tensor(key[:, :], dstf[:, :], float(NT), cst_sb[:, CST_KEY:CST_KEY + TILES],
                                                ALU.mult, ALU.add))
            then(nc.vector.tensor_tensor(key[:, :], key[:, :], chunk[:, :], ALU.add))
            nc.vector.tensor_scalar(out_lo[:, :], key[:, :], 0.0, None, ALU.is_lt).then_inc(edges_ready, 1)

            def add_region(i, r):
                dve.wait_ge(region_ps, i * 2 + r + 1)
                dve.wait_ge(region_added, i * 2 + r + 2)
                cols_ = A[:, :, bass.ds(i * (2 * STEP) + r * STEP, REG_NODES)]
                nc.vector.tensor_tensor(cols_, cols_, ps[0:R, r, 0:REG_COLS].rearrange("p (d c) -> p c d", c=NT),
                                        ALU.add).then_inc(region_added, 1)

            dve.wait_ge(adj_zeroed, 1)
            with dve.Fori(0, REGIONS // 2) as i:
                for j in range(2 * TILES_REG):
                    if j == TILES_REG + 2 * SLOTS:
                        add_region(i, 0)
                    t = i * (2 * TILES_REG) + j
                    dve.wait_ge(slot_free, t + 1)
                    nc.vector.tensor_scalar(oh_src[:, j % SLOTS, :], iota[:, 0:R], srow[:, bass.ds(t, 1)], None,
                                            ALU.is_equal).then_inc(src_ready, 1)
                    nc.vector.tensor_scalar(oh_dst[:, j % SLOTS, :], iota[:, 0:KEYS], key[:, bass.ds(t, 1)],
                                            w_sb[:, bass.ds(t, 1)], ALU.is_equal, ALU.mult).then_inc(dst_ready, 1)
                add_region(i, 1)

            then(nc.vector.scalar_tensor_tensor(out_win[:, :], key[:, :], float(KEYS), out_lo[:, :], ALU.is_ge, ALU.add))
            nc.vector.tensor_tensor(w_out[:, :], out_win[:, :], w_sb[:, :], ALU.mult)
            nc.vector.reduce_max(any_p[:, :], out_win[:, 0:REAL_TILES], AX.X).then_inc(any_ready, 1)

            dve.wait_ge(rows_in, 16)
            for t in range(NT):
                dve.wait_ge(qkv_ps, t + 1)
                nc.vector.tensor_tensor(qkv[:, t, 0:512], ps[0:R, 4 + 2 * (t % 2), 0:512],
                                        rows_sb[0:R, ROW_BQKV:ROW_BQKV + 512], ALU.add)
                nc.vector.tensor_tensor(qkv[:, t, 512:768], ps[0:R, 5 + 2 * (t % 2), 0:256],
                                        rows_sb[0:R, ROW_BQKV + 512:ROW_BQKV + 768], ALU.add).then_inc(qkv_ready, 1)
            dve.wait_ge(qkv_ready, NT)
            then(nc.vector.tensor_tensor(sq[:, :, :], qkv[:, :, 0:512], qkv[:, :, 0:512], ALU.mult))
            nc.vector.tensor_reduce(ss[:, :, :], sq[:, :, :].rearrange("p t (h d) -> p t h d", d=D),
                                    AX.X, ALU.add).then_inc(ss_ready, 1)
            nc.vector.tensor_scalar(temp2[:, :], rows_sb[0:R, ROW_TEMP:ROW_TEMP + H], SCALE2, None, ALU.mult)
            dve.wait_ge(nrm_ready, 2)
            then(nc.vector.tensor_scalar(nrm[:, :, :], nrm[:, :, :], 1e-12, None, ALU.max))
            then(nc.vector.reciprocal(nrm[:, :, :], nrm[:, :, :]))
            nc.vector.tensor_tensor(nrm[:, :, 0:H], nrm[:, :, 0:H],
                                    temp2[:, :].unsqueeze(1).to_broadcast([R, NT, H]), ALU.mult)
            then(nc.vector.tensor_scalar(nrm[:, :, H:2 * H], nrm[:, :, H:2 * H], SCALE, None, ALU.mult))
            for t in range(NT):
                nc.vector.tensor_tensor(qkv[:, t, 0:512].rearrange("p (h d) -> p h d", d=D),
                                        qkv[:, t, 0:512].rearrange("p (h d) -> p h d", d=D),
                                        nrm[:, t, :].unsqueeze(2).to_broadcast([R, 2 * H, D]),
                                        ALU.mult).then_inc(qk_normed, 1)

            dve.wait_ge(vsum_ps, 1)
            nc.vector.tensor_copy(vrest[:, :], ps[:, 1, 0:KC]).then_inc(vrest_ready, 1)
            dve.wait_ge(vrest_ready, 1)

            dve.wait_ge(flag_max, 1)
            nc.vector.tensor_copy(flag[:, :], any_all[:, :]).then_inc(flag_ready, 1)
            dve.wait_ge(flag_ready, 1)
            anyf = dve.value_load(flag[0:1, 0:1], min_val=0, max_val=1)
            with dve.If(anyf > 0):
                dve.sem_inc(full_used, 1)
                for c in range(NT):
                    nc.vector.tensor_scalar(in_chunk[:, :], chunk[:, :], float(c), None,
                                            ALU.is_equal).then_inc(chunk_set, 1)
                    dve.wait_ge(chunk_set, 2 * c + 1)
                    nc.vector.tensor_tensor(in_chunk[:, :], in_chunk[:, :], w_out[:, :], ALU.mult).then_inc(chunk_set, 1)
                    dve.wait_ge(chunk_set, 2 * c + 2)
                    with dve.Fori(0, TILES) as t:
                        dve.wait_ge(full_used, t + (c * TILES + 1))
                        nc.vector.tensor_scalar(full_dst[:, 0:N], cst_sb[:, CST_DST:CST_DST + N],
                                                dstf[:, bass.ds(t, 1)], None, ALU.is_equal)
                        nc.vector.tensor_scalar(full_src[:, :], iota[:, 0:R], srow[:, bass.ds(t, 1)],
                                                in_chunk[:, bass.ds(t, 1)], ALU.is_equal,
                                                ALU.mult).then_inc(full_ready, 1)
                    dve.wait_ge(full_ps, c + 1)
                    for a, n0, n1 in ((0, 0, HALF), (1, HALF, N)):
                        nc.vector.tensor_tensor(A[:, c, BEFORE + n0:BEFORE + n1], A[:, c, BEFORE + n0:BEFORE + n1],
                                                ps[0:R, a, 0:n1 - n0], ALU.add).then_inc(full_added, 1)
            nc.vector.tensor_scalar(eps1[:, :], rows_sb[:, ROW_EPS:ROW_EPS + 1], 1.0, None, ALU.add).then_inc(adj_ready, 1)
            dve.wait_ge(adj_ready, 1)


            def combine(grp):
                g, half = grp // 2, grp % 2
                dve.wait_ge(pv_done, NT * (grp + 1))
                then(nc.vector.tensor_scalar(rden[:, :], ps[:, 3, 0:HALF], REST * N, None, ALU.add))
                then(nc.vector.reciprocal(rden[:, :], rden[:, :]))
                nc.vector.scalar_tensor_tensor(yT[:, g, half * HALF:(half + 1) * HALF], ps[:, 2, 0:HALF],
                                               vrest[:, g:g + 1], rden[:, :], ALU.add, ALU.mult).then_inc(y_ready, 1)

            def aggregate():
                for m in range(KC):
                    dve.wait_ge(agg_ps, m + 1)
                    nc.vector.scalar_tensor_tensor(gT[:, m, :].rearrange("p (a n) -> p a n", a=2),
                                                   xnT[:, m, :].rearrange("p (a n) -> p a n", a=2), eps1[:, :],
                                                   ps[:, 0:2, 0:HALF], ALU.mult, ALU.add).then_inc(agg_ready, 1)

            def batch_norm(layer, dst, gcol, becol):
                for m in range(KC):
                    dve.wait_ge(lin_ready, layer * KC + m + 1)
                    nc.vector.bn_stats(bst[:, m, 0, :], hT[:, m, 0:HALF])
                    last = nc.vector.bn_stats(bst[:, m, 1, :], hT[:, m, HALF:N])
                then(last)
                for m in range(KC):
                    last = nc.vector.bn_aggr(bmv[:, m, :], bst[:, m, :, :])
                last.then_inc(bvar_ready, 1)
                dve.wait_ge(bstd_ready, layer + 1)
                then(nc.vector.reciprocal(bscale[:, :], bstd[:, :]))
                then(nc.vector.tensor_tensor(bscale[:, :], bscale[:, :], cols_sb[:, gcol:gcol + KC], ALU.mult))
                then(nc.vector.tensor_tensor(btmp[:, :], bmv[:, :, 0], bscale[:, :], ALU.mult))
                then(nc.vector.tensor_tensor(bshift[:, :], cols_sb[:, becol:becol + KC], btmp[:, :], ALU.subtract))
                for m in range(KC):
                    last = nc.vector.tensor_scalar(dst[:, m, :], hT[:, m, :], bscale[:, m:m + 1], bshift[:, m:m + 1],
                                                   ALU.mult, ALU.add)
                last.then_inc(bn_ready, 1)

            dve.wait_ge(cols_in, 16)
            aggregate()
            combine(0)
            batch_norm(0, uT, COL["gg1"], COL["gbe1"])
            combine(1)
            batch_norm(1, gT, COL["gg2"], COL["gbe2"])
            combine(2)
            for t in range(NT):
                last = nc.vector.tensor_tensor(acc[:, t, :], x_sb[:, t, :], rows_sb[0:R, ROW_BPROJ:ROW_BPROJ + C], ALU.add)
            then(last)
            combine(3)
            for t in range(NT):
                dve.wait_ge(mix_ps, t + 1)
                nc.vector.tensor_tensor(acc[:, t, :], acc[:, t, :], ps[0:R, 2 + t % 4, 0:C],
                                        ALU.add).then_inc(mix_added, 1)
            dve.wait_ge(mix_added, NT)

            row_norm(acc, x2n, x2n_ready, 1)

            dve.wait_ge(gate_ps, 1)
            then(nc.vector.tensor_tensor(prob[:, :, :], ps[0:R, 7, 0:NT * NX].rearrange("p (t e) -> p t e", t=NT),
                                         rows_sb[0:R, ROW_GB:ROW_GB + NX].unsqueeze(1).to_broadcast([R, NT, NX]),
                                         ALU.add))

            def per_row(op_out, a, b, op):
                then(nc.vector.tensor_tensor(op_out, a, b[:, :].unsqueeze(2).to_broadcast([R, NT, NX]), op))

            then(nc.vector.tensor_reduce(red[:, :], prob[:, :, :], AX.X, ALU.max))
            nc.vector.tensor_tensor(prob[:, :, :], prob[:, :, :], red[:, :].unsqueeze(2).to_broadcast([R, NT, NX]),
                                    ALU.subtract).then_inc(logits_ready, 1)
            dve.wait_ge(exp_ready, 1)
            then(nc.vector.tensor_reduce(red[:, :], prob[:, :, :], AX.X, ALU.add))
            then(nc.vector.reciprocal(red[:, :], red[:, :]))
            per_row(prob[:, :, :], prob[:, :, :], red, ALU.mult)
            rank = cst_sb[0:R, CST_RANK:CST_RANK + NX].unsqueeze(1).to_broadcast([R, NT, NX])

            def first_max(src, dst):
                then(nc.vector.tensor_reduce(red[:, :], src[:, :, :], AX.X, ALU.max))
                per_row(rank1[:, :, :], src[:, :, :], red, ALU.is_equal)
                then(nc.vector.tensor_tensor(rank1[:, :, :], rank1[:, :, :], rank, ALU.mult))
                then(nc.vector.tensor_reduce(red[:, :], rank1[:, :, :], AX.X, ALU.max))
                per_row(dst[:, :, :], rank1[:, :, :], red, ALU.is_equal)

            first_max(prob, top1)
            then(nc.vector.scalar_tensor_tensor(rest[:, :, :], top1[:, :, :], -2.0, prob[:, :, :], ALU.mult, ALU.add))
            first_max(rest, top2)
            then(nc.vector.tensor_tensor(top1[:, :, :], top1[:, :, :], top2[:, :, :], ALU.add))
            then(nc.vector.tensor_tensor(cw[:, :, :], top1[:, :, :], prob[:, :, :], ALU.mult))
            nc.vector.tensor_copy(cwe[:, :, :], cw[:, :, :].rearrange("p t e -> p e t")).then_inc(cw_ready, 1)
            dve.wait_ge(cwT_ps, 1)
            nc.vector.tensor_copy(cwT[:, 0:4 * R], ps[0:NX, 7, 0:4 * R])
            nc.vector.tensor_copy(cwT[:, 4 * R:N], ps[0:NX, 6, 0:R]).then_inc(cwT_ready, 1)
            for t in range(NT):
                dve.wait_ge(bias_ps, t + 1)
                nc.vector.tensor_tensor(acc[:, t, :], acc[:, t, :],
                                        ps[0:R, 4 + t % 4, 0:C], ALU.add).then_inc(down_added, 1)

            with dve.Fori(0, NX // 2) as i:
                for s in range(2):
                    for t in range(NT):
                        dve.wait_ge(down_ps, i * (2 * NT) + (s * NT + t + 1))
                        wcol = cwe[:, :, :].rearrange("p e t -> p (e t)")[:, bass.ds(i * (2 * NT) + (s * NT + t), 1)]
                        nc.vector.scalar_tensor_tensor(acc[:, t, :], ps[0:R, 4 + t % 4, 0:C],
                                                       wcol, acc[:, t, :], ALU.mult, ALU.add).then_inc(down_added, 1)

        @block.tensor
        def _(pe):
            pe.sem_inc(slot_free, SLOTS)
            pe.sem_inc(region_added, 2)
            pe.sem_inc(gelu_ready, 2)
            pe.wait_ge(cst_in, 16)
            pe.wait_ge(consts_set, 8)

            for t in range(NT):
                pe.wait_ge(xn_ready, t + 1)
                if t >= 2:
                    pe.wait_ge(xT_ready, t - 1)
                for m in range(KC):
                    last = nc.tensor.transpose(ps[:, 2 + t % 2, m * R:(m + 1) * R],
                                               xn[:, t, m * 128:(m + 1) * 128], ident[0:R, 0:R])
                last.then_inc(xT_ps, 1)

            pe.wait_ge(wqkv_in, 16)

            def project(t):
                pe.wait_ge(xT_ready, t + 1)
                if t >= 2:
                    pe.wait_ge(qkv_ready, t - 1)
                for a, n0, n1 in ((0, 0, 512), (1, 512, 768)):
                    for k in range(KC):
                        last = nc.tensor.matmul(ps[0:R, 4 + 2 * (t % 2) + a, 0:n1 - n0],
                                                xnT[:, k, t * R:(t + 1) * R], wqkv_sb[:, k, n0:n1],
                                                start=(k == 0), stop=(k == KC - 1))
                last.then_inc(qkv_ps, 1)

            project(0)
            project(1)

            with pe.Fori(0, REGIONS // 2) as i:
                for r in range(2):
                    pe.wait_ge(region_added, i * 2 + r + 1)
                    nc.tensor.matmul(ps[0:R, r, 0:REG_COLS], zeros[:, 0:R], zeros[:, 0:REG_COLS],
                                     start=True, stop=False, skip_group_check=True)
                    for j in range(TILES_REG):
                        n = r * TILES_REG + j
                        pe.wait_ge(src_ready, i * (2 * TILES_REG) + (n + 1))
                        pe.wait_ge(dst_ready, i * (2 * TILES_REG) + (n + 1))
                        last = nc.tensor.matmul(ps[0:R, r, TILE_OFF[j] * NT:TILE_OFF[j] * NT + KEYS],
                                                oh_src[:, n % SLOTS, :], oh_dst[:, n % SLOTS, :],
                                                start=False, stop=(j == TILES_REG - 1), skip_group_check=True)
                        last.then_inc(slot_free, 1)
                    nc.tensor.matmul(ps[0:R, r, 0:REG_COLS], zeros[:, 0:R], zeros[:, 0:REG_COLS],
                                     start=False, stop=True, skip_group_check=True).then_inc(region_ps, 1)

            for t in range(2, NT):
                project(t)
            for t in range(NT):
                pe.wait_ge(qk_normed, t + 1)
                if t >= 2:
                    pe.wait_ge(qkT_ready, 2 * (t - 1))
                for a in range(2):
                    for m in range(KC):
                        last = nc.tensor.transpose(ps[:, 2 + t % 2, (a * KC + m) * R:(a * KC + m + 1) * R],
                                                   qkv[:, t, a * C + m * 128:a * C + (m + 1) * 128], ident[0:R, 0:R])
                last.then_inc(qkT_ps, 1)

            pe.wait_ge(region_added, REGIONS + 2)
            for g in range(KC):
                for t in range(NT):
                    last = nc.tensor.matmul(ps[:, 1, g:g + 1], qkv[:, t, 512 + g * 128:512 + (g + 1) * 128],
                                            rest_c[0:R, :], start=(t == 0), stop=(t == NT - 1))
            last.then_inc(vsum_ps, 1)
            pe.wait_ge(vrest_ready, 1)
            pe.wait_ge(flag_ready, 1)
            anyf = pe.value_load(flag[0:1, 0:1], min_val=0, max_val=1)
            with pe.If(anyf > 0):
                for c in range(NT):
                    if c:
                        pe.wait_ge(full_added, 2 * c)
                    for a in range(2):
                        nc.tensor.matmul(ps[0:R, a, 0:HALF], zeros[:, 0:R], zeros[:, 0:HALF],
                                         start=True, stop=False, skip_group_check=True)
                    with pe.Fori(0, TILES) as t:
                        pe.wait_ge(full_ready, t + (c * TILES + 1))
                        for a, n0, n1 in ((0, 0, HALF), (1, HALF, N)):
                            last = nc.tensor.matmul(ps[0:R, a, 0:n1 - n0], full_src[:, :], full_dst[:, n0:n1],
                                                    start=False, stop=False, skip_group_check=True)
                        last.then_inc(full_used, 1)
                    for a in range(2):
                        last = nc.tensor.matmul(ps[0:R, a, 0:HALF], zeros[:, 0:R], zeros[:, 0:HALF],
                                                start=False, stop=True, skip_group_check=True)
                    last.then_inc(full_ps, 1)

            def scores(u):
                g, half, kt = u // (2 * NT), (u // NT) % 2, u % NT
                if u == 0:
                    pe.wait_ge(qkT_ready, 2 * NT)
                for j in range(4):
                    if j % 2 == 0 and u >= 1:
                        pe.wait_ge(squares_ready, 2 * (u - 1) + j // 2 + 1)
                    last = nc.tensor.matmul(ps[0:R, 4 + j, 0:HALF], kT[32 * j:32 * j + 32, g, kt * R:(kt + 1) * R],
                                            qT[32 * j:32 * j + 32, g, half * HALF:(half + 1) * HALF],
                                            start=True, stop=True, tile_position=(32 * j, 0))
                    if j % 2 == 1:
                        last.then_inc(scores_ready, 1)

            def weigh(u):
                g, kt = u // (2 * NT), u % NT
                pe.wait_ge(squares_ready, 2 * (u + 1))
                if kt == 0 and u:
                    pe.wait_ge(y_ready, u // NT)
                for bank, lhs in ((2, None), (3, ones)):
                    for j in range(4):
                        w = ones[0:R, :] if lhs is ones else qkv[:, kt, 512 + g * 128 + 32 * j:512 + g * 128 + 32 * j + 32]
                        last = nc.tensor.matmul(ps[32 * j:32 * j + 32, bank, 0:HALF], w, P[:, u % 2, j, :],
                                                start=(kt == 0), stop=(kt == NT - 1), tile_position=(0, 32 * j))
                last.then_inc(pv_done, 1)

            def aggregate(m):
                if m == 0:
                    pe.wait_ge(adj_ready, 1)
                else:
                    pe.wait_ge(agg_ready, m)
                for a in range(2):
                    for c in range(NT):
                        last = nc.tensor.matmul(ps[:, a, 0:HALF], xn[:, c, m * 128:(m + 1) * 128],
                                                A[:, c, BEFORE + a * HALF:BEFORE + (a + 1) * HALF],
                                                start=(c == 0), stop=(c == NT - 1))
                last.then_inc(agg_ps, 1)

            def linear(layer, w, src, m):
                if m == 0:
                    pe.wait_ge(wsmall_in, 80)
                    pe.wait_ge(agg_ready, KC)
                    if layer:
                        pe.wait_ge(bn_ready, layer)
                        pe.wait_ge(lin_ready, KC)
                else:
                    pe.wait_ge(lin_ready, layer * KC + m)
                for a in range(2):
                    for k in range(KC):
                        last = nc.tensor.matmul(ps[:, a, 0:HALF], w[:, k, m * 128:(m + 1) * 128],
                                                src[:, k, a * HALF:(a + 1) * HALF], start=(k == 0), stop=(k == KC - 1))
                last.then_inc(lin_ps, 1)

            between = {1: lambda: aggregate(0), 2: lambda: aggregate(1),
                       3: lambda: linear(0, gw1_sb, gT, 0), 4: lambda: linear(0, gw1_sb, gT, 1),
                       8: lambda: linear(1, gw2_sb, uT, 0), 9: lambda: linear(1, gw2_sb, uT, 1)}
            scores(0)
            for u in range(UNITS):
                if u + 1 < UNITS:
                    scores(u + 1)
                weigh(u)
                if u in between:
                    between[u]()

            pe.wait_ge(y_ready, 4)
            pe.wait_ge(bn_ready, 2)
            for t in range(NT):
                if t == 4:
                    pe.wait_ge(mix_added, 1)
                o = ps[0:R, 2 + t % 4, 0:C]
                for k in range(KC):
                    nc.tensor.matmul(o, yT[:, k, t * R:(t + 1) * R], wproj_sb[:, k, :], start=(k == 0), stop=False,
                                     skip_group_check=True)
                for m in range(KC):
                    last = nc.tensor.matmul(o[:, m * 128:(m + 1) * 128], gT[:, m, t * R:(t + 1) * R], ident,
                                            start=False, stop=(m == KC - 1), skip_group_check=True)
                last.then_inc(mix_ps, 1)

            for t in range(NT):
                pe.wait_ge(x2n_ready, t + 1)
                if t >= 2:
                    pe.wait_ge(x2T_ready, t - 1)
                for m in range(KC):
                    last = nc.tensor.transpose(ps[:, t % 2, m * R:(m + 1) * R],
                                               x2n[:, t, m * 128:(m + 1) * 128], ident[0:R, 0:R])
                last.then_inc(x2T_ps, 1)

            pe.wait_ge(x2T_ready, NT)
            for t in range(NT):
                for k in range(KC):
                    last = nc.tensor.matmul(ps[0:R, 7, t * NX:(t + 1) * NX], x2T[:, k, t * R:(t + 1) * R],
                                            gatew_sb[:, k, :], start=(k == 0), stop=(k == KC - 1))
            last.then_inc(gate_ps, 1)
            pe.wait_ge(cw_ready, 1)
            for t in range(NT):
                o = ps[0:NX, 7, t * R:(t + 1) * R] if t < 4 else ps[0:NX, 6, 0:R]
                last = nc.tensor.transpose(o, cw[:, t, :], ident[0:R, 0:R])
            last.then_inc(cwT_ps, 1)
            pe.wait_ge(cwT_ready, 1)
            for t in range(NT):
                if t == 4:
                    pe.wait_ge(down_added, 1)
                nc.tensor.matmul(ps[0:R, 4 + t % 4, 0:C], cwT[:, t * R:(t + 1) * R],
                                 fb2_sb[:, :], start=True, stop=True).then_inc(bias_ps, 1)

            with pe.Fori(0, NX // 2) as i:
                for s in range(2):
                    pe.wait_ge(fw_in[s], i * 32 + 32)
                    for m in range(MC):
                        g = s * MC + m
                        pe.wait_ge(gelu_ready, i * (2 * MC) + (g + 1))
                        for k in range(KC):
                            for a in range(2):
                                last = nc.tensor.matmul(ps[:, 2 * (m % 2) + a, 0:HALF],
                                                        fw1_sb[:, s, k, m * 128:(m + 1) * 128],
                                                        x2T[:, k, a * HALF:(a + 1) * HALF],
                                                        start=(k == 0), stop=(k == KC - 1))
                        last.then_inc(up_ps, 1)
                    pe.wait_ge(gelu_ready, i * (2 * MC) + ((s + 1) * MC + 2))
                    for t in range(NT):
                        if t == 0 or t == 4:
                            pe.wait_ge(down_added, i * (2 * NT) + (s * NT + NT + t // 4))
                        for k in range(MC):
                            last = nc.tensor.matmul(ps[0:R, 4 + t % 4, 0:C],
                                                    act_h[:, s, k, t * R:(t + 1) * R], fw2_sb[:, s, k, :],
                                                    start=(k == 0), stop=(k == MC - 1))
                        last.then_inc(down_ps, 1)


def kernel(**inputs):
    import numpy as np
    import concourse.bacc as bacc
    from concourse.bass_utils import run_bass_kernel_spmd

    a = {k: np.asarray(v) for k, v in inputs.items()}
    f32 = np.float32

    def edge_tiles(v, fill):
        pad = np.full(TILES * 128, fill, v.dtype)
        pad[:E] = v
        return np.ascontiguousarray(pad.reshape(TILES, 128).T)

    cst = np.zeros((128, CSTS), f32)
    cst[:, CST_ID:CST_ID + 128] = np.eye(128, dtype=f32)
    cst[:, CST_IOTA:CST_IOTA + 128] = np.arange(128, dtype=f32)
    first = [STEP * (t // TILES_REG) + TILE_OFF[t % TILES_REG] for t in range(TILES)]
    cst[:, CST_KEY:CST_KEY + TILES] = np.array([NT * (BEFORE - f) for f in first], f32)
    cst[:, CST_RANK:CST_RANK + NX] = np.arange(NX, 0, -1, dtype=f32)
    cst[:, CST_DST:CST_DST + N] = np.arange(N, dtype=f32)

    def by_partition(v):
        return v.reshape(-1, 128).T

    cols = np.concatenate([by_partition(a["L0_gnn_" + k]) for k in ("b1", "g1", "be1", "b2", "g2", "be2")]
                          + [by_partition(a["L0_ffn_b1"].reshape(-1))], axis=1)
    rows = np.concatenate([a["L0_mix_bqkv"], a["L0_mix_bproj"], a["L0_ffn_gate_b"],
                           a["L0_mix_temperature"].reshape(-1), a["L0_gnn_eps"]])
    arrays = {
        "x": a["x"], "esrc": edge_tiles(a["src"], 0), "edst": edge_tiles(a["dst"], N - 1),
        "ew": edge_tiles(a["edge_weight"], 0), "cst": cst, "cols": cols, "rows": rows,
        "wqkvT": a["L0_mix_Wqkv"].T, "wprojT": a["L0_mix_Wproj"].T, "gw1": a["L0_gnn_W1"], "gw2": a["L0_gnn_W2"],
        "gatew": a["L0_ffn_gate_w"], "fw1": a["L0_ffn_W1"], "fw2": a["L0_ffn_W2"], "fb2": a["L0_ffn_b2"],
    }
    arrays = {k + "_dram": np.ascontiguousarray(v) for k, v in arrays.items()}
    nc = bacc.Bacc("TRN2", target_bir_lowering=False, num_devices=1)
    args = [nc.dram_tensor(k, v.shape, mybir.dt.from_np(v.dtype), kind="ExternalInput").ap() for k, v in arrays.items()]
    out = nc.dram_tensor("out_dram", (N, C), F32, kind="ExternalOutput").ap()
    graph_layer(nc, *args, out)
    r = run_bass_kernel_spmd(nc, [arrays], core_ids=[0])
    return r.results[0]["out_dram"]
```

```python
from contextlib import ExitStack

import concourse.bass as bass
from concourse import mybir

F32 = mybir.dt.float32
BF16 = mybir.dt.bfloat16
F16 = mybir.dt.float16
I32 = mybir.dt.int32
ALU = mybir.AluOpType
ACT = mybir.ActivationFunctionType
AX = mybir.AxisListType
RMAX = bass.bass_isa.ReduceOp.max

N = 625
H, D = 8, 32
D1 = D + 1
C = 256
NT, R = 5, 125
KC = C // 128
HALF = 313
NP = 2 * HALF
E = 20625
NX, HID = 8, 512
MC = HID // 128
XTILES = (2 * N - NX) // 128 + NX
XTILES_MIN = -(-2 * N // 128)
SCRATCH = XTILES + 2
EXPERT = KC * HID + MC * C
LN_EPS = 1e-5

GROUP = 7
GROUPS = 3
TILES_REG = GROUP * GROUPS
REGIONS = H
TILES = TILES_REG * REGIONS
REAL_TILES = -(-E // 128)
STEP = 81
WIN = 18
BEFORE = 6
KEYS = WIN * NT
TILE_OFF = [(j * 128 * N) // E for j in range(TILES_REG)]
REG_NODES = TILE_OFF[-1] + WIN
REG_COLS = REG_NODES * NT
AW = STEP * (REGIONS - 1) + REG_NODES

COL = {n: i for i, n in enumerate(["gb1", "gb1_", "gg1", "gg1_", "gbe1", "gbe1_",
                                   "gb2", "gb2_", "gg2", "gg2_", "gbe2", "gbe2_"])}
COL_FB1 = 12
COLS = COL_FB1 + NX * MC
ROW_BQKV, ROW_BPROJ, ROW_GB, ROW_TEMP, ROW_EPS = 0, 768, 1024, 1032, 1040
ROWS = 1041
CST_ID, CST_IOTA, CST_KEY = 0, 128, 256
CST_RANK = CST_KEY + TILES
CST_DST = CST_RANK + NX
CST_TRI = CST_DST + N
CST_THR = CST_TRI + 128
CST_LT = CST_THR + NT
CST_G = CST_LT + NX * NX
CSTS = CST_G + XTILES

SCALE2 = float(D) ** 0.5
SCALE = float(D) ** 0.25
SHIFT = SCALE2
REST = 2.0 * (float(D) - 0.5 * SCALE2 * SCALE2)


def graph_layer(nc, x, esrc, edst, ew, cst, cols, rows, wqkvT, wprojT, gw1, gw2, gatew, fw1, fw2, fb2, out):
    with ExitStack() as ctx:
        def sb(name, shape, dt=F32):
            return ctx.enter_context(nc.sbuf_tensor(name, shape, dt))

        def sem(name):
            return ctx.enter_context(nc.semaphore(name))

        ps = ctx.enter_context(nc.psum_tensor("ps", [128, 8, 512], F32))
        ps16 = ps[:, :, :].bitcast(F16)
        TS = R + 1

        x_sb = sb("x_sb", [R, NT, C])
        cst_sb = sb("cst_sb", [128, CSTS])
        cols_sb = sb("cols_sb", [128, COLS])
        rows_sb = sb("rows_sb", [128, ROWS])
        src_i = sb("src_i", [128, TILES], I32)
        dst_i = sb("dst_i", [128, TILES], I32)
        w_sb = sb("w_sb", [128, TILES])
        wqkv_sb = sb("wqkv_sb", [128, KC, 3 * C])
        wproj_sb = sb("wproj_sb", [128, KC, C])
        gw1_sb = sb("gw1_sb", [128, KC, C])
        gw2_sb = sb("gw2_sb", [128, KC, C])
        gatew_sb = sb("gatew_sb", [128, KC, NX])
        fb2_sb = sb("fb2_sb", [NX, C])
        arena = sb("arena", [128, max(NX * EXPERT, 2 * EXPERT + 2 * NT * NP + TILES_REG * (R + 2 * KEYS))])
        W_WORK = 2 * EXPERT
        W_OH = W_WORK + 2 * NT * NP
        ident = cst_sb[:, CST_ID:CST_ID + 128]
        iota = cst_sb[:, CST_IOTA:CST_IOTA + 128]
        ident16 = sb("ident16", [128, 128], F16)

        stats = sb("stats", [128, NT, 6])
        mv = sb("mv", [128, NT, 2])
        std = sb("std", [128, NT])
        rstd = sb("rstd", [128, NT])
        xn = sb("xn", [R, NT, C])
        xnT = sb("xnT", [128, KC, NP])
        eps_c = sb("eps_c", [128, 1])
        shift_c = sb("shift_c", [128, 1])
        ones = sb("ones", [128, 32])
        rest_c = sb("rest_c", [128, R])
        zeros = sb("zeros", [128, 512], BF16)

        srcf = sb("srcf", [128, TILES])
        dstf = sb("dstf", [128, TILES])
        chunk = sb("chunk", [128, TILES])
        srow = sb("srow", [128, TILES])
        key = sb("key", [128, TILES])
        out_lo = sb("out_lo", [128, TILES])
        out_win = sb("out_win", [128, TILES])
        w_out = sb("w_out", [128, TILES])
        any_p = sb("any_p", [128, 1])
        any_all = sb("any_all", [128, 1])
        flag = sb("flag", [128, 1], I32)
        ohs = arena[:, W_OH:W_OH + TILES_REG * (R + 2 * KEYS)]
        oh_src = ohs[:, 0:TILES_REG * R].rearrange("p (g q r) -> p g q r", g=GROUPS, q=GROUP)
        oh_key = ohs[:, TILES_REG * R:TILES_REG * (R + KEYS)].rearrange("p (g q k) -> p g q k", g=GROUPS, q=GROUP)
        oh_dst = ohs[:, TILES_REG * (R + KEYS):].rearrange("p (g q k) -> p g q k", g=GROUPS, q=GROUP)
        A = sb("A", [R, NT, AW])
        full_dst = oh_key[:, 0:1].rearrange("p g q k -> p (g q k)")
        full_src = sb("full_src", [128, R])
        in_chunk = sb("in_chunk", [128, TILES])

        qk = sb("qk", [R, NT, 2 * C])
        v1 = sb("v1", [R, NT, H, D1])
        ss = sb("ss", [R, NT, 2 * H])
        nrm = sb("nrm", [R, NT, 2 * H])
        qT = sb("qT", [128, H, NP], F16)
        kT = sb("kT", [128, H, NP], F16)
        work = arena[:, W_WORK:W_OH]
        sq = work[0:R, 0:NT * 2 * C].rearrange("p (t c) -> p t c", t=NT)
        split = work[0:R, 0:NT * 4 * C].bitcast(F16).rearrange("p (t a h s d) -> p t a h s d", t=NT, a=2, h=H, s=4)
        P = work[0:R, :].rearrange("p (s k n) -> p s k n", s=2, k=NT)
        temp = sb("temp", [128, 2])
        vrest = sb("vrest", [R, H * D1])
        ysum = sb("ysum", [R, 2, NT, D1])
        rden = sb("rden", [R, 2, NT])
        y = sb("y", [R, NT, C])
        yT = sb("yT", [128, KC, NP])

        eps1 = sb("eps1", [128, 1])
        gT = sb("gT", [128, KC, NP])
        hT = sb("hT", [128, KC, NP])
        bst = sb("bst", [128, KC, 2, 6])
        bmv = sb("bmv", [128, KC, 2])
        bstd = sb("bstd", [128, KC])
        bscale = sb("bscale", [128, KC])
        bshift = sb("bshift", [128, KC])
        btmp = sb("btmp", [128, KC])
        uT = sb("uT", [128, KC, NP])

        acc = sb("acc", [R, NT, C])
        x2n = y
        x2T = xnT
        prob = sb("prob", [R, NT, NX])
        red = sb("red", [R, NT])
        rank1 = sb("rank1", [R, NT, NX])
        tops = sb("tops", [R, 2, NT, NX])
        top1, top2 = tops[:, 0], tops[:, 1]
        rest = sb("rest", [R, NT, NX])
        cw = sb("cw", [R, NT, NX])
        pair = sb("pair", [R, 2, NT, NX])
        wtop = sb("wtop", [R, 2, NT])
        sel = sb("sel", [R, NT, NX], BF16)
        tri = sb("tri", [128, 128], BF16)
        ones16 = sb("ones16", [128, 128], BF16)
        tiles_gt = sb("tiles_gt", [R, NX, NT])
        tiles_e = sb("tiles_e", [R, NX])
        before = sb("before", [R, NX, NX])
        base_e = sb("base_e", [R, NX])
        slot_e = sb("slot_e", [R, NT, NX])
        slot_f = sb("slot_f", [R, 2, NT])
        slot_i = sb("slot_i", [R, 2, NT], I32)
        end_e = sb("end_e", [R, NX])
        past = sb("past", [R, XTILES, NX])
        meta = sb("meta", [R, XTILES + 1])
        meta_i = sb("meta_i", [R, XTILES + 1], I32)
        warm = sb("warm", [128, 1])
        x_rows = sb("x_rows", [128, C])
        xT_t = sb("xT_t", [128, KC, 128])
        h_rows = sb("h_rows", [128, HID])
        hT_t = sb("hT_t", [128, MC, 128])
        y_rows = sb("y_rows", [128, C])
        got = qk[:, :, :].rearrange("p t (j c) -> p t j c", j=2)
        cwT = sb("cwT", [NX, N])

        cst_in, rows_in, cols_in, edges_in = (sem(n) for n in ("cst_in", "rows_in", "cols_in", "edges_in"))
        x_in = [sem(f"x_in{t}") for t in range(NT)]
        wqkv_in, wsmall_in = sem("wqkv_in"), sem("wsmall_in")
        fw_in = sem("fw_in")
        scratch_zeroed, scattered, tile_in, y_written, out_done = (
            sem(n) for n in ("scratch_zeroed", "scattered", "tile_in", "y_written", "out_done"))
        all_loaded, all_written = sem("all_loaded"), sem("all_written")
        gathered = [sem(f"gathered{t}") for t in range(NT)]
        consts_set = sem("consts_set")
        dve_step = sem("dve_step")
        ln_var, ln_std, xn_ready = sem("ln_var"), sem("ln_std"), sem("xn_ready")
        xT_ps, xT_ready = sem("xT_ps"), sem("xT_ready")
        qkv_ps, qkv_ready = sem("qkv_ps"), sem("qkv_ready")
        sq_ready, ss_ready, nrm_ready, qk_normed, hi_ready, lo_ready, split_ready = (
            sem(n) for n in ("sq_ready", "ss_ready", "nrm_ready", "qk_normed", "hi_ready", "lo_ready", "split_ready"))
        qkT_ps, qkT_ready = sem("qkT_ps"), sem("qkT_ready")
        vsum_ps, vrest_ready = sem("vsum_ps"), sem("vrest_ready")
        any_ready, flag_max, flag_ready = (sem(n) for n in ("any_ready", "flag_max", "flag_ready"))
        group_free, src_ready, key_ready, dst_ready = (sem(n) for n in ("group_free", "src_ready", "key_ready", "dst_ready"))
        region_ps, region_added = sem("region_ps"), sem("region_added")
        full_ready, full_used, full_ps, full_added = (sem(n) for n in ("full_ready", "full_used", "full_ps", "full_added"))
        adj_zeroed, adj_ready, chunk_set = sem("adj_zeroed"), sem("adj_ready"), sem("chunk_set")
        scores_ready, squares_ready, pv_done, head_step, y_ready, yT_ps, yT_ready = (
            sem(n) for n in ("scores_ready", "squares_ready", "pv_done", "head_step", "y_ready", "yT_ps", "yT_ready"))
        temp_ready, warmed = sem("temp_ready"), sem("warmed")
        agg_ps, agg_ready = sem("agg_ps"), sem("agg_ready")
        lin_ps, lin_ready, bvar_ready, bstd_ready, bn_ready = (
            sem(n) for n in ("lin_ps", "lin_ready", "bvar_ready", "bstd_ready", "bn_ready"))
        mix_ps, mix_added = sem("mix_ps"), sem("mix_added")
        x2n_ready, x2T_ps, x2T_ready = sem("x2n_ready"), sem("x2T_ps"), sem("x2T_ready")
        gate_ps, logits_ready, exp_ready, cw_ready = sem("gate_ps"), sem("logits_ready"), sem("exp_ready"), sem("cw_ready")
        cwT_ps, cwT_ready, bias_ps = sem("cwT_ps"), sem("cwT_ready"), sem("bias_ps")
        sel_ready, rank_ps, slots_ready, meta_ready, bias_added = (
            sem(n) for n in ("sel_ready", "rank_ps", "slots_ready", "meta_ready", "bias_added"))
        x_turned, xT_copied, up_ps, up_copied, h_turned, gelu_ready, down_ps, y_copied, tile_added = (
            sem(n) for n in ("x_turned", "xT_copied", "up_ps", "up_copied", "h_turned", "gelu_ready", "down_ps",
                             "y_copied", "tile_added"))

        x_slots = nc.dram_tensor("x_slots", (SCRATCH * 128, C), F32, kind="Internal").ap()
        y_slots = nc.dram_tensor("y_slots", (XTILES * 128, C), F32, kind="Internal").ap()
        MIX = (2, 3, 6, 7, 2)

        block = ctx.enter_context(nc.Block())

        @block.sync
        def _(sp):
            for t in range(NT):
                sp.dma_start(x_sb[:, t, :], x[t * R:(t + 1) * R, :]).then_inc(x_in[t], 16)
            sp.dma_start(src_i[:, :], esrc[:, :]).then_inc(edges_in, 16)
            sp.dma_start(dst_i[:, :], edst[:, :]).then_inc(edges_in, 16)
            sp.dma_start(w_sb[:, :], ew[:, :]).then_inc(edges_in, 16)
            sp.dma_start(wqkv_sb[:, :, :], wqkvT.rearrange("(k p) n -> p k n", p=128)).then_inc(wqkv_in, 16)
            sp.dma_start(cols_sb[:, :], cols[:, :]).then_inc(cols_in, 16)
            for dst, src in ((wproj_sb, wprojT), (gw1_sb, gw1), (gw2_sb, gw2), (gatew_sb, gatew)):
                sp.dma_start(dst[:, :, :], src.rearrange("(k p) n -> p k n", p=128)).then_inc(wsmall_in, 16)
            sp.dma_start(fb2_sb[:, :], fb2[:, :]).then_inc(wsmall_in, 16)
            def expert(e):
                sp.dma_start(arena[:, e * EXPERT:e * EXPERT + KC * HID].rearrange("p (k n) -> p k n", k=KC),
                             fw1[e].rearrange("(k p) n -> p k n", p=128)).then_inc(fw_in, 16)
                sp.dma_start(arena[:, e * EXPERT + KC * HID:(e + 1) * EXPERT].rearrange("p (k n) -> p k n", k=MC),
                             fw2[e].rearrange("(k p) n -> p k n", p=128)).then_inc(fw_in, 16)

            expert(0)
            expert(1)
            sp.wait_ge(adj_ready, 1)
            sp.wait_ge(pv_done, H + 2)
            for e in range(2, NX):
                expert(e)

            for slots, n in ((x_slots, SCRATCH), (y_slots, XTILES)):
                sp.dma_start(slots.rearrange("(g p) c -> p g c", p=128),
                             zeros[:, :].bitcast(F32).unsqueeze(1).to_broadcast([128, n, C])).then_inc(scratch_zeroed, 16)

            sp.wait_ge(scattered, 16 * 2 * NT)
            sp.wait_ge(meta_ready, 1)
            n_tiles = sp.value_load(meta_i[0:1, XTILES:XTILES + 1], min_val=XTILES_MIN, max_val=XTILES)

            def load(g, before_it):
                if before_it is not None:
                    sp.wait_ge(x_turned, before_it)
                sp.dma_start(x_rows[:, :], x_slots[bass.ds(g * 128, 128), :]).then_inc(tile_in, 16)

            def store(g):
                sp.wait_ge(y_copied, g + 2)
                sp.dma_start(y_slots[bass.ds(g * 128, 128), :], y_rows[:, :]).then_inc(y_written, 16)

            load(0, None)
            load(1, 1)
            load(2, 2)
            with sp.Fori(0, n_tiles - 1) as g:
                load(g + 3, g + 3)
                store(g)
            store(n_tiles - 1)
            sp.wait_ge(tile_in, n_tiles * 16 + 32)
            sp.sem_inc(all_loaded, 1)
            sp.wait_ge(y_written, n_tiles * 16 + 16)
            sp.sem_inc(all_written, 1)
            for t in range(NT):
                sp.wait_ge(tile_added, t + 1)
                sp.dma_start(out[t * R:(t + 1) * R, :], acc[:, t, :]).then_inc(out_done, 16)
            sp.wait_ge(out_done, 16 * NT)

        @block.gpsimd
        def _(pool):
            nc.gpsimd.memset(A[:, :, :], 0.0).then_inc(adj_zeroed, 1)
            for t in range(NT):
                pool.wait_ge(lo_ready, t + 1)
                nc.gpsimd.tensor_copy(split[:, t, 0, :, 2, :], split[:, t, 0, :, 1, :])
                nc.gpsimd.tensor_copy(split[:, t, 1, :, 3, :], split[:, t, 1, :, 1, :]).then_inc(split_ready, 1)

            pool.wait_ge(edges_in, 48)
            with pool.Fori(0, H // 2) as i:
                for n in range(2 * GROUPS):
                    g = n % GROUPS
                    pool.wait_ge(key_ready, i * (2 * GROUPS) + (n + 1))
                    pool.wait_ge(group_free, i * (2 * GROUPS) + (n + 1))
                    wt = w_sb[:, bass.ds(i * (2 * TILES_REG) + n * GROUP, GROUP)]
                    nc.gpsimd.tensor_tensor(oh_dst[:, g], oh_key[:, g], wt.unsqueeze(2).to_broadcast([128, GROUP, KEYS]),
                                            ALU.mult).then_inc(dst_ready, 1)
            pool.wait_ge(any_ready, 1)
            nc.gpsimd.partition_all_reduce(any_all[:, :], any_p[:, :], 128, RMAX).then_inc(flag_max, 1)

            pool.wait_ge(slots_ready, 1)
            pool.wait_ge(x2n_ready, NT)
            pool.wait_ge(scratch_zeroed, 32)
            for t in range(NT):
                for j in range(2):
                    nc.gpsimd.indirect_dma_start(
                        out=x_slots[:, :], out_offset=bass.IndirectOffsetOnAxis(ap=slot_i[:, j, t:t + 1], axis=0),
                        in_=x2n[:, t, :], in_offset=None).then_inc(scattered, 16)
            pool.wait_ge(all_written, 1)
            for t in range(NT):
                for j in range(2):
                    nc.gpsimd.indirect_dma_start(
                        out=got[:, t, j, :], out_offset=None, in_=y_slots[:, :],
                        in_offset=bass.IndirectOffsetOnAxis(ap=slot_i[:, j, t:t + 1], axis=0)).then_inc(gathered[t], 16)

        @block.scalar
        def _(act):
            act.dma_start(cst_sb[:, :], cst[:, :]).then_inc(cst_in, 16)
            act.dma_start(rows_sb[:, :], rows.partition_broadcast(128)).then_inc(rows_in, 16)

            act.wait_ge(consts_set, 8)
            act.wait_ge(ln_var, 1)
            nc.scalar.activation(std[0:R, :], mv[0:R, :, 1], ACT.Sqrt, bias=eps_c[0:R, :]).then_inc(ln_std, 1)

            for t in range(NT):
                act.wait_ge(xT_ps, t + 1)
                nc.scalar.copy(xnT[:, :, t * R:(t + 1) * R],
                               ps[:, 2 + t % 2, 0:KC * R].rearrange("p (m r) -> p m r", m=KC)).then_inc(xT_ready, 1)

            for t in range(NT):
                act.wait_ge(qkv_ready, t + 1)
                nc.scalar.activation(sq[:, t, :], qk[:, t, :], ACT.Square).then_inc(sq_ready, 1)
            act.wait_ge(ss_ready, 1)
            nc.scalar.activation(nrm[:, :, 0:H], ss[:, :, 0:H], ACT.Sqrt, scale=SCALE2).then_inc(nrm_ready, 1)
            nc.scalar.activation(nrm[:, :, H:2 * H], ss[:, :, H:2 * H], ACT.Sqrt).then_inc(nrm_ready, 1)
            for t in range(NT):
                act.wait_ge(qk_normed, t + 1)
                for a in range(2):
                    nc.scalar.copy(split[:, t, a, :, 0::3 - a, :][:, :, 0:2],
                                   qk[:, t, a * C:(a + 1) * C].rearrange("p (h d) -> p h d", d=D)
                                   .unsqueeze(2).to_broadcast([R, H, 2, D])).then_inc(hi_ready, 1)

            for t in range(NT):
                act.wait_ge(qkT_ps, t + 1)
                for a, buf in ((0, qT), (1, kT)):
                    bank = ps16[:, 2 * (t % 2) + a, 0:H * TS].rearrange("p (h r) -> p h r", h=H)
                    nc.scalar.copy(buf[:, :, t * R:(t + 1) * R], bank[:, :, 0:R]).then_inc(qkT_ready, 1)

            act.wait_ge(rows_in, 16)
            with act.Fori(0, H // 2) as i:
                for s in range(2):
                    nc.scalar.copy(temp[0:R, s:s + 1],
                                   rows_sb[0:R, bass.ds(i * 2 + (ROW_TEMP + s), 1)]).then_inc(temp_ready, 1)
                    act.wait_ge(temp_ready, i * 2 + (s + 1))
                    act.wait_ge(pv_done, i * 2 + (s + 1))
                    for kt in range(NT):
                        u = s * NT + kt
                        act.wait_ge(scores_ready, i * (2 * NT) + (u + 1))
                        nc.scalar.activation(P[:, s, kt, :].rearrange("p (a n) -> p a n", a=2),
                                             ps[0:R, 2 + 2 * (u % 2):4 + 2 * (u % 2), 0:HALF], ACT.Square,
                                             bias=shift_c[0:R, :], scale=temp[0:R, s:s + 1]).then_inc(squares_ready, 1)

            def y_out():
                for t in range(NT):
                    act.wait_ge(yT_ps, t + 1)
                    nc.scalar.copy(yT[:, :, t * R:(t + 1) * R],
                                   ps[:, 2 + t % 2, 0:KC * R].rearrange("p (m r) -> p m r", m=KC)).then_inc(yT_ready, 1)

            def linear_out(layer):
                for m in range(KC):
                    act.wait_ge(lin_ps, layer * KC + m + 1)
                    if layer == 1 and m == 0:
                        act.wait_ge(bn_ready, 1)
                    b = cols_sb[:, (COL["gb1"] if layer == 0 else COL["gb2"]) + m:][:, 0:1]
                    nc.scalar.activation(hT[:, m, :].rearrange("p (a n) -> p a n", a=2), ps[:, 4 * m:4 * m + 2, 0:HALF],
                                         ACT.Identity, bias=b).then_inc(lin_ready, 1)

            def bn_std(layer):
                act.wait_ge(bvar_ready, layer + 1)
                nc.scalar.activation(bstd[:, :], bmv[:, :, 1], ACT.Sqrt, bias=eps_c[:, :]).then_inc(bstd_ready, 1)

            act.wait_ge(cols_in, 16)
            y_out()
            linear_out(0)
            bn_std(0)
            linear_out(1)
            bn_std(1)

            act.wait_ge(ln_var, 2)
            nc.scalar.activation(std[0:R, :], mv[0:R, :, 1], ACT.Sqrt, bias=eps_c[0:R, :]).then_inc(ln_std, 1)
            for t in range(NT):
                act.wait_ge(x2T_ps, t + 1)
                nc.scalar.copy(x2T[:, :, t * R:(t + 1) * R],
                               ps[:, t % 2, 0:KC * R].rearrange("p (m r) -> p m r", m=KC)).then_inc(x2T_ready, 1)

            act.wait_ge(logits_ready, 1)
            nc.scalar.activation(prob[:, :, :], prob[:, :, :], ACT.Exp).then_inc(exp_ready, 1)

            act.wait_ge(meta_ready, 1)
            n_tiles = act.value_load(meta_i[0:1, XTILES:XTILES + 1], min_val=XTILES_MIN, max_val=XTILES)

            def gelu(g):
                e = act.value_load(meta_i[0:1, bass.ds(g, 1)], min_val=0, max_val=NX - 1)
                nc.scalar.activation(warm[:, :], eps_c[:, :], ACT.Gelu).then_inc(warmed, 1)
                act.wait_ge(warmed, g + 1)
                act.wait_ge(h_turned, g + 1)
                for m in range(MC):
                    b = cols_sb[:, bass.ds(e * MC + (COL_FB1 + m), 1)]
                    nc.scalar.activation(hT_t[:, m, :], ps[:, 1, m * 128:(m + 1) * 128], ACT.Gelu,
                                         bias=b).then_inc(gelu_ready, 1)

            with act.Fori(0, n_tiles - 1) as g:
                gelu(g)
            gelu(n_tiles - 1)

        @block.vector
        def _(dve):
            steps = [0]

            def then(ins):
                steps[0] += 1
                ins.then_inc(dve_step, 1)
                dve.wait_ge(dve_step, steps[0])

            nc.vector.memset(eps_c[:, :], LN_EPS).then_inc(consts_set, 1)
            nc.vector.memset(zeros[:, :], 0.0).then_inc(consts_set, 1)
            nc.vector.memset(shift_c[:, :], SHIFT).then_inc(consts_set, 1)
            nc.vector.memset(ones[:, :], 1.0).then_inc(consts_set, 1)
            nc.vector.memset(rest_c[:, :], REST).then_inc(consts_set, 1)
            for buf in (xnT, qT):
                nc.vector.memset(buf[:, :, N:NP], 0.0).then_inc(consts_set, 1)
            nc.vector.memset(v1[:, :, :, D:D1].rearrange("p t h o -> p t (h o)"), 1.0).then_inc(consts_set, 1)
            dve.wait_ge(consts_set, 8)

            def row_norm(src, dst, ready, layer):
                for t in range(NT):
                    if layer == 0:
                        dve.wait_ge(x_in[t], 16)
                    last = nc.vector.bn_stats(stats[0:R, t, :], src[:, t, :])
                then(last)
                for t in range(NT):
                    last = nc.vector.bn_aggr(mv[0:R, t, :], stats[0:R, t, :])
                last.then_inc(ln_var, 1)
                dve.wait_ge(ln_std, layer + 1)
                then(nc.vector.reciprocal(rstd[0:R, :], std[0:R, :]))
                for t in range(NT):
                    nc.vector.tensor_scalar(dst[:, t, :], src[:, t, :], mv[0:R, t, 0:1], rstd[0:R, t:t + 1],
                                            ALU.subtract, ALU.mult).then_inc(ready, 1)

            row_norm(x_sb, xn, xn_ready, 0)

            dve.wait_ge(edges_in, 48)
            dve.wait_ge(cst_in, 16)
            nc.vector.tensor_copy(ident16[:, :], ident)
            nc.vector.tensor_copy(tri[:, :], cst_sb[:, CST_TRI:CST_TRI + 128])
            nc.vector.memset(ones16[:, :], 1.0)
            nc.vector.tensor_copy(srcf[:, :], src_i[:, :])
            then(nc.vector.tensor_copy(dstf[:, :], dst_i[:, :]))
            then(nc.vector.tensor_scalar(chunk[:, :], srcf[:, :], float(R), None, ALU.is_ge))
            for c in range(2, NT):
                then(nc.vector.scalar_tensor_tensor(chunk[:, :], srcf[:, :], float(c * R), chunk[:, :],
                                                    ALU.is_ge, ALU.add))
            nc.vector.scalar_tensor_tensor(srow[:, :], chunk[:, :], -float(R), srcf[:, :], ALU.mult, ALU.add)
            then(nc.vector.scalar_tensor_tensor(key[:, :], dstf[:, :], float(NT), cst_sb[:, CST_KEY:CST_KEY + TILES],
                                                ALU.mult, ALU.add))
            then(nc.vector.tensor_tensor(key[:, :], key[:, :], chunk[:, :], ALU.add))
            then(nc.vector.tensor_scalar(out_lo[:, :], key[:, :], 0.0, None, ALU.is_lt))

            then(nc.vector.scalar_tensor_tensor(out_win[:, :], key[:, :], float(KEYS), out_lo[:, :], ALU.is_ge, ALU.add))
            nc.vector.tensor_tensor(w_out[:, :], out_win[:, :], w_sb[:, :], ALU.mult)
            nc.vector.reduce_max(any_p[:, :], out_win[:, 0:REAL_TILES], AX.X).then_inc(any_ready, 1)

            dve.wait_ge(rows_in, 16)
            for t in range(NT):
                dve.wait_ge(qkv_ps, t + 1)
                nc.vector.tensor_tensor(qk[:, t, :], ps[0:R, 4 + 2 * (t % 2), 0:512],
                                        rows_sb[0:R, ROW_BQKV:ROW_BQKV + 512], ALU.add)
                nc.vector.tensor_tensor(v1[:, t, :, 0:D],
                                        ps[0:R, 5 + 2 * (t % 2), 0:256].rearrange("p (h d) -> p h d", d=D),
                                        rows_sb[0:R, ROW_BQKV + 512:ROW_BQKV + 768].rearrange("p (h d) -> p h d", d=D),
                                        ALU.add).then_inc(qkv_ready, 1)
            for t in range(NT):
                dve.wait_ge(sq_ready, t + 1)
                last = nc.vector.tensor_reduce(ss[:, t, :], sq[:, t, :].rearrange("p (h d) -> p h d", d=D), AX.X, ALU.add)
            last.then_inc(ss_ready, 1)
            dve.wait_ge(nrm_ready, 2)
            then(nc.vector.tensor_scalar(nrm[:, :, :], nrm[:, :, :], 1e-12, None, ALU.max))
            then(nc.vector.reciprocal(nrm[:, :, :], nrm[:, :, :]))
            nc.vector.tensor_scalar(nrm[:, :, 0:H], nrm[:, :, 0:H], SCALE2, None, ALU.mult)
            then(nc.vector.tensor_scalar(nrm[:, :, H:2 * H], nrm[:, :, H:2 * H], SCALE, None, ALU.mult))
            for t in range(NT):
                rows3 = qk[:, t, :].rearrange("p (h d) -> p h d", d=D)
                nc.vector.tensor_tensor(rows3, rows3, nrm[:, t, :].unsqueeze(2).to_broadcast([R, 2 * H, D]),
                                        ALU.mult).then_inc(qk_normed, 1)
            for t in range(NT):
                dve.wait_ge(hi_ready, 2 * (t + 1))
                parts = split[:, t].rearrange("p a h s d -> p (a h) s d")
                nc.vector.tensor_tensor(parts[:, :, 1, :], qk[:, t, :].rearrange("p (a d) -> p a d", d=D),
                                        parts[:, :, 0, :], ALU.subtract).then_inc(lo_ready, 1)
            dve.wait_ge(vsum_ps, 1)
            nc.vector.tensor_copy(vrest[:, :], ps[0:R, 4, 0:H * D1]).then_inc(vrest_ready, 1)
            dve.wait_ge(vrest_ready, 1)

            def add_region(i, r):
                dve.wait_ge(region_ps, i * 2 + (r + 1))
                dve.wait_ge(region_added, i * 2 + (r + 2))
                span = A[:, :, bass.ds(i * (2 * STEP) + r * STEP, REG_NODES)]
                nc.vector.tensor_tensor(span, span, ps[0:R, r, 0:REG_COLS].rearrange("p (d c) -> p c d", c=NT),
                                        ALU.add).then_inc(region_added, 1)

            def head_rows(i, s):
                dve.wait_ge(pv_done, i * 2 + (s + 3))
                vr = vrest[:, bass.ds(i * (2 * D1) + s * D1, D1)]
                nc.vector.tensor_tensor(ysum[:, s], ps[0:R, 6 + s, 0:NT * D1].rearrange("p (t d) -> p t d", d=D1),
                                        vr.unsqueeze(1).to_broadcast([R, NT, D1]), ALU.add).then_inc(head_step, 1)
                dve.wait_ge(head_step, i * 4 + (2 * s + 1))
                nc.vector.reciprocal(rden[:, s, :], ysum[:, s, :, D]).then_inc(head_step, 1)
                dve.wait_ge(head_step, i * 4 + (2 * s + 2))
                nc.vector.tensor_tensor(y[:, :, bass.ds(i * (2 * D) + s * D, D)], ysum[:, s, :, 0:D],
                                        rden[:, s, :].unsqueeze(2).to_broadcast([R, NT, D]), ALU.mult).then_inc(y_ready, 1)

            dve.wait_ge(adj_zeroed, 1)

            def one_hots(i, s):
                for g in range(GROUPS):
                    n = s * GROUPS + g
                    dve.wait_ge(group_free, i * (2 * GROUPS) + (n + 1))
                    tiles = bass.ds(i * (2 * TILES_REG) + n * GROUP, GROUP)
                    nc.vector.tensor_tensor(oh_key[:, g], iota[:, 0:KEYS].unsqueeze(1).to_broadcast([128, GROUP, KEYS]),
                                            key[:, tiles].unsqueeze(2).to_broadcast([128, GROUP, KEYS]),
                                            ALU.is_equal).then_inc(key_ready, 1)
                    nc.vector.tensor_tensor(oh_src[:, g], iota[:, 0:R].unsqueeze(1).to_broadcast([128, GROUP, R]),
                                            srow[:, tiles].unsqueeze(2).to_broadcast([128, GROUP, R]),
                                            ALU.is_equal).then_inc(src_ready, 1)

            one_hots(0, 0)
            with dve.Fori(0, H // 2 - 1) as i:
                one_hots(i, 1)
                add_region(i, 0)
                head_rows(i, 0)
                one_hots(i + 1, 0)
                add_region(i, 1)
                head_rows(i, 1)
            one_hots(H // 2 - 1, 1)
            for s in range(2):
                add_region(H // 2 - 1, s)
                head_rows(H // 2 - 1, s)

            dve.wait_ge(flag_max, 1)
            nc.vector.tensor_copy(flag[:, :], any_all[:, :]).then_inc(flag_ready, 1)
            dve.wait_ge(flag_ready, 1)
            anyf = dve.value_load(flag[0:1, 0:1], min_val=0, max_val=1)
            with dve.If(anyf > 0):
                dve.sem_inc(full_used, 1)
                for c in range(NT):
                    nc.vector.tensor_scalar(in_chunk[:, :], chunk[:, :], float(c), None,
                                            ALU.is_equal).then_inc(chunk_set, 1)
                    dve.wait_ge(chunk_set, 2 * c + 1)
                    nc.vector.tensor_tensor(in_chunk[:, :], in_chunk[:, :], w_out[:, :], ALU.mult).then_inc(chunk_set, 1)
                    dve.wait_ge(chunk_set, 2 * c + 2)
                    with dve.Fori(0, TILES) as t:
                        dve.wait_ge(full_used, t + (c * TILES + 1))
                        nc.vector.tensor_scalar(full_dst[:, 0:N], cst_sb[:, CST_DST:CST_DST + N],
                                                dstf[:, bass.ds(t, 1)], None, ALU.is_equal)
                        nc.vector.tensor_scalar(full_src[:, :], iota[:, 0:R], srow[:, bass.ds(t, 1)],
                                                in_chunk[:, bass.ds(t, 1)], ALU.is_equal,
                                                ALU.mult).then_inc(full_ready, 1)
                    dve.wait_ge(full_ps, c + 1)
                    for a, n0, n1 in ((0, 0, HALF), (1, HALF, N)):
                        nc.vector.tensor_tensor(A[:, c, BEFORE + n0:BEFORE + n1], A[:, c, BEFORE + n0:BEFORE + n1],
                                                ps[0:R, a, 0:n1 - n0], ALU.add).then_inc(full_added, 1)
            nc.vector.tensor_scalar(eps1[:, :], rows_sb[:, ROW_EPS:ROW_EPS + 1], 1.0, None, ALU.add).then_inc(adj_ready, 1)
            dve.wait_ge(adj_ready, 1)


            def aggregate():
                for m in range(KC):
                    dve.wait_ge(agg_ps, m + 1)
                    nc.vector.scalar_tensor_tensor(gT[:, m, :].rearrange("p (a n) -> p a n", a=2),
                                                   xnT[:, m, :].rearrange("p (a n) -> p a n", a=2), eps1[:, :],
                                                   ps[:, 4 * m:4 * m + 2, 0:HALF], ALU.mult, ALU.add).then_inc(agg_ready, 1)

            def batch_norm(layer, dst, gcol, becol):
                for m in range(KC):
                    dve.wait_ge(lin_ready, layer * KC + m + 1)
                    nc.vector.bn_stats(bst[:, m, 0, :], hT[:, m, 0:HALF])
                    last = nc.vector.bn_stats(bst[:, m, 1, :], hT[:, m, HALF:N])
                then(last)
                for m in range(KC):
                    last = nc.vector.bn_aggr(bmv[:, m, :], bst[:, m, :, :])
                last.then_inc(bvar_ready, 1)
                dve.wait_ge(bstd_ready, layer + 1)
                then(nc.vector.reciprocal(bscale[:, :], bstd[:, :]))
                then(nc.vector.tensor_tensor(bscale[:, :], bscale[:, :], cols_sb[:, gcol:gcol + KC], ALU.mult))
                then(nc.vector.tensor_tensor(btmp[:, :], bmv[:, :, 0], bscale[:, :], ALU.mult))
                then(nc.vector.tensor_tensor(bshift[:, :], cols_sb[:, becol:becol + KC], btmp[:, :], ALU.subtract))
                for m in range(KC):
                    last = nc.vector.tensor_scalar(dst[:, m, :], hT[:, m, :], bscale[:, m:m + 1], bshift[:, m:m + 1],
                                                   ALU.mult, ALU.add)
                last.then_inc(bn_ready, 1)

            dve.wait_ge(cols_in, 16)
            aggregate()
            for t in range(NT):
                last = nc.vector.tensor_tensor(acc[:, t, :], x_sb[:, t, :], rows_sb[0:R, ROW_BPROJ:ROW_BPROJ + C], ALU.add)
            then(last)
            batch_norm(0, uT, COL["gg1"], COL["gbe1"])
            batch_norm(1, gT, COL["gg2"], COL["gbe2"])
            for t in range(NT):
                dve.wait_ge(mix_ps, t + 1)
                nc.vector.tensor_tensor(acc[:, t, :], acc[:, t, :], ps[0:R, MIX[t], 0:C],
                                        ALU.add).then_inc(mix_added, 1)
            dve.wait_ge(mix_added, NT)

            row_norm(acc, x2n, x2n_ready, 1)

            dve.wait_ge(gate_ps, 1)
            then(nc.vector.tensor_tensor(prob[:, :, :], ps[0:R, 7, 0:NT * NX].rearrange("p (t e) -> p t e", t=NT),
                                         rows_sb[0:R, ROW_GB:ROW_GB + NX].unsqueeze(1).to_broadcast([R, NT, NX]),
                                         ALU.add))

            def per_row(op_out, a, b, op):
                then(nc.vector.tensor_tensor(op_out, a, b[:, :].unsqueeze(2).to_broadcast([R, NT, NX]), op))

            then(nc.vector.tensor_reduce(red[:, :], prob[:, :, :], AX.X, ALU.max))
            nc.vector.tensor_tensor(prob[:, :, :], prob[:, :, :], red[:, :].unsqueeze(2).to_broadcast([R, NT, NX]),
                                    ALU.subtract).then_inc(logits_ready, 1)
            dve.wait_ge(exp_ready, 1)
            then(nc.vector.tensor_reduce(red[:, :], prob[:, :, :], AX.X, ALU.add))
            then(nc.vector.reciprocal(red[:, :], red[:, :]))
            per_row(prob[:, :, :], prob[:, :, :], red, ALU.mult)
            rank = cst_sb[0:R, CST_RANK:CST_RANK + NX].unsqueeze(1).to_broadcast([R, NT, NX])

            def first_max(src, dst):
                then(nc.vector.tensor_reduce(red[:, :], src[:, :, :], AX.X, ALU.max))
                per_row(rank1[:, :, :], src[:, :, :], red, ALU.is_equal)
                then(nc.vector.tensor_tensor(rank1[:, :, :], rank1[:, :, :], rank, ALU.mult))
                then(nc.vector.tensor_reduce(red[:, :], rank1[:, :, :], AX.X, ALU.max))
                per_row(dst[:, :, :], rank1[:, :, :], red, ALU.is_equal)

            first_max(prob, top1)
            then(nc.vector.scalar_tensor_tensor(rest[:, :, :], top1[:, :, :], -2.0, prob[:, :, :], ALU.mult, ALU.add))
            first_max(rest, top2)
            nc.vector.tensor_tensor(sel[:, :, :], top1, top2, ALU.add).then_inc(sel_ready, 1)
            then(nc.vector.tensor_tensor(pair[:, :, :, :].rearrange("p j t e -> p j (t e)"),
                                         tops[:, :, :, :].rearrange("p j t e -> p j (t e)"),
                                         prob[:, :, :].rearrange("p t e -> p (t e)").unsqueeze(1)
                                         .to_broadcast([R, 2, NT * NX]), ALU.mult))
            nc.vector.tensor_tensor(cw[:, :, :], pair[:, 0], pair[:, 1], ALU.add).then_inc(cw_ready, 1)
            then(nc.vector.tensor_reduce(wtop[:, :, :], pair[:, :, :, :], AX.X, ALU.add))
            dve.wait_ge(rank_ps, 1)
            then(nc.vector.tensor_tensor(tiles_gt[:, :, :],
                                         ps[0:R, 5, NT * NX:(NT + 1) * NX].unsqueeze(2).to_broadcast([R, NX, NT]),
                                         cst_sb[0:R, CST_THR:CST_THR + NT].unsqueeze(1).to_broadcast([R, NX, NT]),
                                         ALU.is_gt))
            then(nc.vector.tensor_reduce(tiles_e[:, :], tiles_gt[:, :, :], AX.X, ALU.add))
            then(nc.vector.tensor_tensor(before[:, :, :], tiles_e[:, :].unsqueeze(1).to_broadcast([R, NX, NX]),
                                         cst_sb[0:R, CST_LT:CST_LT + NX * NX].rearrange("p (a b) -> p a b", a=NX),
                                         ALU.mult))
            then(nc.vector.tensor_reduce(base_e[:, :], before[:, :, :], AX.X, ALU.add))
            then(nc.vector.scalar_tensor_tensor(slot_e[:, :, :], base_e[:, :].unsqueeze(1).to_broadcast([R, NT, NX]),
                                                128.0, ps[0:R, 5, 0:NT * NX].rearrange("p (t e) -> p t e", t=NT),
                                                ALU.mult, ALU.add))
            then(nc.vector.tensor_tensor(pair[:, :, :, :].rearrange("p j t e -> p j (t e)"),
                                         tops[:, :, :, :].rearrange("p j t e -> p j (t e)"),
                                         slot_e[:, :, :].rearrange("p t e -> p (t e)").unsqueeze(1)
                                         .to_broadcast([R, 2, NT * NX]), ALU.mult))
            then(nc.vector.tensor_reduce(slot_f[:, :, :], pair[:, :, :, :], AX.X, ALU.add))
            nc.vector.tensor_copy(slot_i[:, :, :], slot_f[:, :, :]).then_inc(slots_ready, 1)
            then(nc.vector.tensor_tensor(end_e[:, :], base_e[:, :], tiles_e[:, :], ALU.add))
            then(nc.vector.tensor_tensor(past[:, :, :],
                                         cst_sb[0:R, CST_G:CST_G + XTILES].unsqueeze(2).to_broadcast([R, XTILES, NX]),
                                         end_e[:, :].unsqueeze(1).to_broadcast([R, XTILES, NX]), ALU.is_ge))
            nc.vector.tensor_reduce(meta[:, 0:XTILES], past[:, :, :], AX.X, ALU.add)
            then(nc.vector.tensor_copy(meta[:, XTILES:XTILES + 1], end_e[:, NX - 1:NX]))
            nc.vector.tensor_copy(meta_i[:, :], meta[:, :]).then_inc(meta_ready, 1)
            dve.wait_ge(cwT_ps, 1)
            nc.vector.tensor_copy(cwT[:, 0:4 * R], ps[0:NX, 7, 0:4 * R])
            nc.vector.tensor_copy(cwT[:, 4 * R:N], ps[0:NX, 6, 0:R]).then_inc(cwT_ready, 1)
            for t in range(NT):
                dve.wait_ge(bias_ps, t + 1)
                nc.vector.tensor_tensor(acc[:, t, :], acc[:, t, :], ps[0:R, 4 + t % 4, 0:C],
                                        ALU.add).then_inc(bias_added, 1)

            dve.wait_ge(meta_ready, 1)
            n_tiles = dve.value_load(meta_i[0:1, XTILES:XTILES + 1], min_val=XTILES_MIN, max_val=XTILES)

            def copy_xT(g):
                dve.wait_ge(x_turned, g + 1)
                nc.vector.tensor_copy(xT_t[:, :, :],
                                      ps[:, 2, 0:KC * 128].rearrange("p (m r) -> p m r", m=KC)).then_inc(xT_copied, 1)

            def copy_up(g):
                dve.wait_ge(up_ps, g + 1)
                nc.vector.tensor_copy(h_rows[:, :], ps[:, 0, 0:HID]).then_inc(up_copied, 1)

            def copy_y(g):
                dve.wait_ge(down_ps, g + 1)
                dve.wait_ge(y_written, g * 16 + 16)
                nc.vector.tensor_copy(y_rows[:, :], ps[:, 3, 0:C]).then_inc(y_copied, 1)

            copy_xT(0)
            copy_up(0)
            copy_xT(1)
            with dve.Fori(0, n_tiles - 1) as g:
                copy_up(g + 1)
                copy_xT(g + 2)
                copy_y(g)
            copy_y(n_tiles - 1)

            for t in range(NT):
                dve.wait_ge(gathered[t], 32)
                if t == 0:
                    dve.wait_ge(bias_added, NT)
                then(nc.vector.scalar_tensor_tensor(acc[:, t, :], got[:, t, 0, :], wtop[:, 0, t:t + 1], acc[:, t, :],
                                                    ALU.mult, ALU.add))
                nc.vector.scalar_tensor_tensor(acc[:, t, :], got[:, t, 1, :], wtop[:, 1, t:t + 1], acc[:, t, :],
                                               ALU.mult, ALU.add).then_inc(tile_added, 1)

        @block.tensor
        def _(pe):
            pe.sem_inc(group_free, GROUPS)
            pe.sem_inc(region_added, 2)
            pe.sem_inc(squares_ready, 2)
            pe.sem_inc(pv_done, 2)
            pe.sem_inc(y_written, 16)
            pe.sem_inc(y_copied, 1)
            pe.wait_ge(cst_in, 16)
            pe.wait_ge(consts_set, 8)

            for t in range(NT):
                pe.wait_ge(xn_ready, t + 1)
                if t >= 2:
                    pe.wait_ge(xT_ready, t - 1)
                for m in range(KC):
                    last = nc.tensor.transpose(ps[:, 2 + t % 2, m * R:(m + 1) * R],
                                               xn[:, t, m * 128:(m + 1) * 128], ident[0:R, 0:R])
                last.then_inc(xT_ps, 1)

            pe.wait_ge(wqkv_in, 16)

            def project(t):
                pe.wait_ge(xT_ready, t + 1)
                if t >= 2:
                    pe.wait_ge(qkv_ready, t - 1)
                for a, n0, n1 in ((0, 0, 512), (1, 512, 768)):
                    for k in range(KC):
                        last = nc.tensor.matmul(ps[0:R, 4 + 2 * (t % 2) + a, 0:n1 - n0],
                                                xnT[:, k, t * R:(t + 1) * R], wqkv_sb[:, k, n0:n1],
                                                start=(k == 0), stop=(k == KC - 1))
                last.then_inc(qkv_ps, 1)

            for t in range(NT):
                project(t)

            for t in range(NT):
                pe.wait_ge(split_ready, t + 1)
                if t >= 2:
                    pe.wait_ge(qkT_ready, 2 * (t - 1))
                for a in range(2):
                    for h in range(H):
                        last = nc.tensor.transpose(ps16[:, 2 * (t % 2) + a, h * TS:h * TS + R],
                                                   split[:, t, a, h].rearrange("p s d -> p (s d)"), ident16[0:R, 0:R])
                last.then_inc(qkT_ps, 1)
            for t in range(NT):
                last = nc.tensor.matmul(ps[0:R, 4, 0:H * D1], rest_c[0:R, :],
                                        v1[:, t].rearrange("p h d -> p (h d)"), start=(t == 0), stop=(t == NT - 1))
            last.then_inc(vsum_ps, 1)
            pe.wait_ge(vrest_ready, 1)
            pe.wait_ge(qkT_ready, 2 * NT)

            def scores(i, s, kt):
                u = s * NT + kt
                pe.wait_ge(squares_ready, i * (2 * NT) + (u + 1))
                head = i * 2 + s
                for a in range(2):
                    last = nc.tensor.matmul(ps[0:R, 2 + 2 * (u % 2) + a, 0:HALF],
                                            kT_flat[:, bass.ds(head * NP + kt * R, R)],
                                            qT_flat[:, bass.ds(head * NP + a * HALF, HALF)], start=True, stop=True)
                last.then_inc(scores_ready, 1)

            def edge_group(i, r, g):
                n = r * GROUPS + g
                pe.wait_ge(src_ready, i * (2 * GROUPS) + (n + 1))
                pe.wait_ge(dst_ready, i * (2 * GROUPS) + (n + 1))
                for q in range(GROUP):
                    at = TILE_OFF[g * GROUP + q] * NT
                    last = nc.tensor.matmul(ps[0:R, r, at:at + KEYS], oh_src[:, g, q, :], oh_dst[:, g, q, :],
                                            start=False, stop=False, skip_group_check=True)
                last.then_inc(group_free, 1)

            def weigh(i, s):
                pe.wait_ge(squares_ready, i * (2 * NT) + ((s + 1) * NT + 2))
                for qt in range(NT):
                    for kt in range(NT):
                        last = nc.tensor.matmul(ps[0:R, 6 + s, qt * D1:(qt + 1) * D1], P[:, s, kt, qt * R:(qt + 1) * R],
                                                v1_flat[:, bass.ds(kt * (H * D1) + (i * 2 + s) * D1, D1)],
                                                start=(kt == 0), stop=(kt == NT - 1))
                last.then_inc(pv_done, 1)

            kT_flat = kT[:, :, :].rearrange("p h n -> p (h n)")
            qT_flat = qT[:, :, :].rearrange("p h n -> p (h n)")
            v1_flat = v1[:, :, :, :].rearrange("p t h d -> p (t h d)")
            with pe.Fori(0, H // 2) as i:
                for s in range(2):
                    pe.wait_ge(region_added, i * 2 + (s + 1))
                    nc.tensor.matmul(ps[0:R, s, 0:REG_COLS], zeros[:, 0:R], zeros[:, 0:REG_COLS],
                                     start=True, stop=False, skip_group_check=True)
                    scores(i, s, 0)
                    scores(i, s, 1)
                    edge_group(i, s, 0)
                    scores(i, s, 2)
                    scores(i, s, 3)
                    edge_group(i, s, 1)
                    scores(i, s, 4)
                    edge_group(i, s, 2)
                    nc.tensor.matmul(ps[0:R, s, 0:REG_COLS], zeros[:, 0:R], zeros[:, 0:REG_COLS],
                                     start=False, stop=True, skip_group_check=True).then_inc(region_ps, 1)
                    weigh(i, s)

            pe.wait_ge(region_added, REGIONS + 2)
            pe.wait_ge(flag_ready, 1)
            anyf = pe.value_load(flag[0:1, 0:1], min_val=0, max_val=1)
            with pe.If(anyf > 0):
                for c in range(NT):
                    if c:
                        pe.wait_ge(full_added, 2 * c)
                    for a in range(2):
                        nc.tensor.matmul(ps[0:R, a, 0:HALF], zeros[:, 0:R], zeros[:, 0:HALF],
                                         start=True, stop=False, skip_group_check=True)
                    with pe.Fori(0, TILES) as t:
                        pe.wait_ge(full_ready, t + (c * TILES + 1))
                        for a, n0, n1 in ((0, 0, HALF), (1, HALF, N)):
                            last = nc.tensor.matmul(ps[0:R, a, 0:n1 - n0], full_src[:, :], full_dst[:, n0:n1],
                                                    start=False, stop=False, skip_group_check=True)
                        last.then_inc(full_used, 1)
                    for a in range(2):
                        last = nc.tensor.matmul(ps[0:R, a, 0:HALF], zeros[:, 0:R], zeros[:, 0:HALF],
                                                start=False, stop=True, skip_group_check=True)
                    last.then_inc(full_ps, 1)

            def aggregate(m):
                if m == 0:
                    pe.wait_ge(adj_ready, 1)
                for a in range(2):
                    for c in range(NT):
                        last = nc.tensor.matmul(ps[:, 4 * m + a, 0:HALF], xn[:, c, m * 128:(m + 1) * 128],
                                                A[:, c, BEFORE + a * HALF:BEFORE + (a + 1) * HALF],
                                                start=(c == 0), stop=(c == NT - 1))
                last.then_inc(agg_ps, 1)

            def linear(layer, w, src, m):
                if m == 0:
                    pe.wait_ge(agg_ready, KC)
                    if layer:
                        pe.wait_ge(bn_ready, layer)
                        pe.wait_ge(lin_ready, KC)
                for a in range(2):
                    for k in range(KC):
                        last = nc.tensor.matmul(ps[:, 4 * m + a, 0:HALF], w[:, k, m * 128:(m + 1) * 128],
                                                src[:, k, a * HALF:(a + 1) * HALF], start=(k == 0), stop=(k == KC - 1))
                last.then_inc(lin_ps, 1)

            def mix_attention(t):
                for k in range(KC):
                    nc.tensor.matmul(ps[0:R, MIX[t], 0:C], yT[:, k, t * R:(t + 1) * R], wproj_sb[:, k, :],
                                     start=(k == 0), stop=False, skip_group_check=True)

            def mix_gin(t):
                for m in range(KC):
                    last = nc.tensor.matmul(ps[0:R, MIX[t], m * 128:(m + 1) * 128], gT[:, m, t * R:(t + 1) * R], ident,
                                            start=False, stop=(m == KC - 1), skip_group_check=True)
                last.then_inc(mix_ps, 1)

            aggregate(0)
            aggregate(1)
            pe.wait_ge(wsmall_in, 80)
            pe.wait_ge(y_ready, H)
            for t in range(NT):
                if t >= 2:
                    pe.wait_ge(yT_ready, t - 1)
                for m in range(KC):
                    last = nc.tensor.transpose(ps[:, 2 + t % 2, m * R:(m + 1) * R],
                                               y[:, t, m * 128:(m + 1) * 128], ident[0:R, 0:R])
                last.then_inc(yT_ps, 1)
            for m in range(KC):
                linear(0, gw1_sb, gT, m)
            pe.wait_ge(yT_ready, NT)
            for t in range(2):
                mix_attention(t)
            for m in range(KC):
                linear(1, gw2_sb, uT, m)
            for t in range(2, 4):
                mix_attention(t)
            pe.wait_ge(bn_ready, 2)
            for t in range(NT):
                if t == 4:
                    pe.wait_ge(mix_added, 1)
                    mix_attention(t)
                mix_gin(t)

            for t in range(NT):
                pe.wait_ge(x2n_ready, t + 1)
                if t >= 2:
                    pe.wait_ge(x2T_ready, t - 1)
                for m in range(KC):
                    last = nc.tensor.transpose(ps[:, t % 2, m * R:(m + 1) * R],
                                               x2n[:, t, m * 128:(m + 1) * 128], ident[0:R, 0:R])
                last.then_inc(x2T_ps, 1)

            pe.wait_ge(x2T_ready, NT)
            for t in range(NT):
                for k in range(KC):
                    last = nc.tensor.matmul(ps[0:R, 7, t * NX:(t + 1) * NX], x2T[:, k, t * R:(t + 1) * R],
                                            gatew_sb[:, k, :], start=(k == 0), stop=(k == KC - 1))
            last.then_inc(gate_ps, 1)
            pe.wait_ge(sel_ready, 1)
            nc.tensor.matmul(ps[0:R, 5, 0:NT * NX], tri[0:R, 0:R], sel[:, :, :].rearrange("p t e -> p (t e)"),
                             start=True, stop=False, skip_group_check=True)
            for t in range(NT):
                last = nc.tensor.matmul(ps[0:R, 5, (t + 1) * NX:(NT + 1) * NX].rearrange("p (t e) -> p t e", e=NX),
                                        ones16[0:R, 0:R], sel[:, t:t + 1, :].to_broadcast([R, NT - t, NX]),
                                        start=False, stop=(t == NT - 1), skip_group_check=True)
            last.then_inc(rank_ps, 1)
            pe.wait_ge(cw_ready, 1)
            for t in range(NT):
                o = ps[0:NX, 7, t * R:(t + 1) * R] if t < 4 else ps[0:NX, 6, 0:R]
                last = nc.tensor.transpose(o, cw[:, t, :], ident[0:R, 0:R])
            last.then_inc(cwT_ps, 1)
            pe.wait_ge(cwT_ready, 1)
            for t in range(NT):
                if t == 4:
                    pe.wait_ge(bias_added, 1)
                nc.tensor.matmul(ps[0:R, 4 + t % 4, 0:C], cwT[:, t * R:(t + 1) * R],
                                 fb2_sb[:, :], start=True, stop=True).then_inc(bias_ps, 1)

            pe.wait_ge(meta_ready, 1)
            n_tiles = pe.value_load(meta_i[0:1, XTILES:XTILES + 1], min_val=XTILES_MIN, max_val=XTILES)
            pe.wait_ge(fw_in, 32 * NX)

            def expert_of(g):
                return pe.value_load(meta_i[0:1, bass.ds(g, 1)], min_val=0, max_val=NX - 1)

            def turn_x(g):
                pe.wait_ge(tile_in, g * 16 + 16)
                for k in range(KC):
                    last = nc.tensor.transpose(ps[:, 2, k * 128:(k + 1) * 128], x_rows[:, k * 128:(k + 1) * 128], ident)
                last.then_inc(x_turned, 1)

            def up(g, e):
                pe.wait_ge(xT_copied, g + 1)
                for k in range(KC):
                    last = nc.tensor.matmul(ps[:, 0, 0:HID], xT_t[:, k, :],
                                            arena[:, bass.ds(e * EXPERT + k * HID, HID)],
                                            start=(k == 0), stop=(k == KC - 1))
                last.then_inc(up_ps, 1)

            def turn_h(g):
                pe.wait_ge(up_copied, g + 1)
                for m in range(MC):
                    last = nc.tensor.transpose(ps[:, 1, m * 128:(m + 1) * 128], h_rows[:, m * 128:(m + 1) * 128], ident)
                last.then_inc(h_turned, 1)

            def down(g, e):
                pe.wait_ge(y_copied, g + 1)
                pe.wait_ge(gelu_ready, (g + 1) * MC)
                for m in range(MC):
                    last = nc.tensor.matmul(ps[:, 3, 0:C], hT_t[:, m, :],
                                            arena[:, bass.ds(e * EXPERT + (KC * HID + m * C), C)],
                                            start=(m == 0), stop=(m == MC - 1))
                last.then_inc(down_ps, 1)

            turn_x(0)
            up(0, expert_of(0))
            turn_x(1)
            with pe.Fori(0, n_tiles - 1) as g:
                turn_h(g)
                up(g + 1, expert_of(g + 1))
                turn_x(g + 2)
                down(g, expert_of(g))
            turn_h(n_tiles - 1)
            down(n_tiles - 1, expert_of(n_tiles - 1))


def kernel(**inputs):
    import numpy as np
    import concourse.bacc as bacc
    from concourse.bass_utils import run_bass_kernel_spmd

    a = {k: np.asarray(v) for k, v in inputs.items()}
    f32 = np.float32

    def edge_tiles(v, fill):
        pad = np.full(TILES * 128, fill, v.dtype)
        pad[:E] = v
        return np.ascontiguousarray(pad.reshape(TILES, 128).T)

    cst = np.zeros((128, CSTS), f32)
    cst[:, CST_ID:CST_ID + 128] = np.eye(128, dtype=f32)
    cst[:, CST_IOTA:CST_IOTA + 128] = np.arange(128, dtype=f32)
    first = [STEP * (t // TILES_REG) + TILE_OFF[t % TILES_REG] for t in range(TILES)]
    cst[:, CST_KEY:CST_KEY + TILES] = np.array([NT * (BEFORE - f) for f in first], f32)
    cst[:, CST_RANK:CST_RANK + NX] = np.arange(NX, 0, -1, dtype=f32)
    cst[:, CST_DST:CST_DST + N] = np.arange(N, dtype=f32)
    cst[:, CST_TRI:CST_TRI + 128] = np.triu(np.ones((128, 128), f32), 1)
    cst[:, CST_THR:CST_THR + NT] = 128 * np.arange(NT, dtype=f32)
    cst[:, CST_LT:CST_LT + NX * NX] = np.tril(np.ones((NX, NX), f32), -1).reshape(-1)
    cst[:, CST_G:CST_G + XTILES] = np.arange(XTILES, dtype=f32)

    def by_partition(v):
        return v.reshape(-1, 128).T

    cols = np.concatenate([by_partition(a["L0_gnn_" + k]) for k in ("b1", "g1", "be1", "b2", "g2", "be2")]
                          + [by_partition(a["L0_ffn_b1"].reshape(-1))], axis=1)
    rows = np.concatenate([a["L0_mix_bqkv"], a["L0_mix_bproj"], a["L0_ffn_gate_b"],
                           a["L0_mix_temperature"].reshape(-1), a["L0_gnn_eps"]])
    arrays = {
        "x": a["x"], "esrc": edge_tiles(a["src"], 0), "edst": edge_tiles(a["dst"], N - 1),
        "ew": edge_tiles(a["edge_weight"], 0), "cst": cst, "cols": cols, "rows": rows,
        "wqkvT": a["L0_mix_Wqkv"].T, "wprojT": a["L0_mix_Wproj"].T, "gw1": a["L0_gnn_W1"], "gw2": a["L0_gnn_W2"],
        "gatew": a["L0_ffn_gate_w"], "fw1": a["L0_ffn_W1"], "fw2": a["L0_ffn_W2"], "fb2": a["L0_ffn_b2"],
    }
    arrays = {k + "_dram": np.ascontiguousarray(v) for k, v in arrays.items()}
    nc = bacc.Bacc("TRN2", target_bir_lowering=False, num_devices=1)
    args = [nc.dram_tensor(k, v.shape, mybir.dt.from_np(v.dtype), kind="ExternalInput").ap() for k, v in arrays.items()]
    out = nc.dram_tensor("out_dram", (N, C), F32, kind="ExternalOutput").ap()
    graph_layer(nc, *args, out)
    r = run_bass_kernel_spmd(nc, [arrays], core_ids=[0])
    return r.results[0]["out_dram"]
```

```python
from contextlib import ExitStack

import concourse.bass as bass
from concourse import mybir

F32 = mybir.dt.float32
BF16 = mybir.dt.bfloat16
F16 = mybir.dt.float16
I32 = mybir.dt.int32
ALU = mybir.AluOpType
ACT = mybir.ActivationFunctionType
AX = mybir.AxisListType
RMAX = bass.bass_isa.ReduceOp.max

N = 625
H, D = 8, 32
D1 = D + 1
VP = 3 * D1
C = 256
NT, R = 5, 125
KC = C // 128
HALF = 313
NP = 2 * HALF
PW = 628
E = 20625
NX, HID = 8, 512
MC = HID // 128
XTILES = (2 * N - NX) // 128 + NX
XTILES_MIN = -(-2 * N // 128)
EXPERT = KC * HID + MC * C
LN_EPS = 1e-5
FAR = 3e38

GROUP = 7
GROUPS = 3
TILES_REG = GROUP * GROUPS
REGIONS = H
TILES = TILES_REG * REGIONS
REAL_TILES = -(-E // 128)
STEP = 81
WIN = 18
BEFORE = 6
KEYS = WIN * NT
TILE_OFF = [(j * 128 * N) // E for j in range(TILES_REG)]
REG_NODES = TILE_OFF[-1] + WIN
REG_COLS = REG_NODES * NT
SHARED = REG_NODES - STEP
AW = STEP * (REGIONS - 1) + REG_NODES

COL = {n: i for i, n in enumerate(["gb1", "gb1_", "gg1", "gg1_", "gbe1", "gbe1_",
                                   "gb2", "gb2_", "gg2", "gg2_", "gbe2", "gbe2_"])}
COL_FB1 = 12
COLS = COL_FB1 + NX * MC
ROW_BQKV, ROW_BPROJ, ROW_GB, ROW_TEMP, ROW_EPS = 0, 768, 1024, 1032, 1040
ROWS = 1041
CST_ID, CST_IOTA, CST_KEY = 0, 128, 256
CST_RANK = CST_KEY + TILES
CST_DST = CST_RANK + NX
CST_TRI = CST_DST + N
CST_THR = CST_TRI + 128
CST_LT = CST_THR + NT
CST_G = CST_LT + NX * NX
CST_ROW = CST_G + XTILES
CST_EMPTY = CST_ROW + 2 * NT
CSTS = CST_EMPTY + XTILES

SCALE2 = float(D) ** 0.5
SCALE = float(D) ** 0.25
SHIFT = SCALE2
REST = 2.0 * (float(D) - 0.5 * SCALE2 * SCALE2)


def graph_layer(nc, x, esrc, edst, ew, cst, cols, rows, wqkvT, wprojT, gw1, gw2, gatew, fw1, fw2, fb2, out):
    with ExitStack() as ctx:
        def sb(name, shape, dt=F32):
            return ctx.enter_context(nc.sbuf_tensor(name, shape, dt))

        def sem(name):
            return ctx.enter_context(nc.semaphore(name))

        ps = ctx.enter_context(nc.psum_tensor("ps", [128, 8, 512], F32))
        ps16 = ps[:, :, :].bitcast(F16)
        TS = R + 1

        x_sb = sb("x_sb", [R, NT, C])
        cst_sb = sb("cst_sb", [128, CSTS])
        cols_sb = sb("cols_sb", [128, COLS])
        rows_sb = sb("rows_sb", [128, ROWS])
        src_i = sb("src_i", [128, TILES], I32)
        dst_i = sb("dst_i", [128, TILES], I32)
        w_sb = sb("w_sb", [128, TILES])
        wqkv_sb = sb("wqkv_sb", [128, KC, 3 * C])
        wproj_sb = sb("wproj_sb", [128, KC, C])
        gw1_sb = sb("gw1_sb", [128, KC, C])
        gw2_sb = sb("gw2_sb", [128, KC, C])
        gatew_sb = sb("gatew_sb", [128, KC, NX])
        fb2_sb = sb("fb2_sb", [NX, C])
        arena = sb("arena", [128, max(NX * EXPERT, 2 * EXPERT + 2 * NT * PW + TILES_REG * (R + 2 * KEYS))])
        W_WORK = 2 * EXPERT
        W_OH = W_WORK + 2 * NT * PW
        ident = cst_sb[:, CST_ID:CST_ID + 128]
        iota = cst_sb[:, CST_IOTA:CST_IOTA + 128]
        ident16 = sb("ident16", [128, 128], F16)

        stats = sb("stats", [128, NT, 6])
        mv = sb("mv", [128, NT, 2])
        std = sb("std", [128, NT])
        rstd = sb("rstd", [128, NT])
        xn = sb("xn", [R, NT, C])
        xnT = sb("xnT", [128, KC, NP])
        eps_c = sb("eps_c", [128, 1])
        ones_r = sb("ones_r", [128, R])
        zeros = sb("zeros", [128, 512], BF16)

        srcf = sb("srcf", [128, TILES])
        dstf = sb("dstf", [128, TILES])
        chunk = sb("chunk", [128, TILES])
        srow = sb("srow", [128, TILES])
        key = sb("key", [128, TILES])
        out_lo = sb("out_lo", [128, TILES])
        out_win = sb("out_win", [128, TILES])
        w_out = sb("w_out", [128, TILES])
        any_p = sb("any_p", [128, 1])
        any_all = sb("any_all", [128, 1])
        flag = sb("flag", [128, 1], I32)
        ohs = arena[:, W_OH:W_OH + TILES_REG * (R + 2 * KEYS)]
        oh_src = ohs[:, 0:TILES_REG * R].rearrange("p (g q r) -> p g q r", g=GROUPS, q=GROUP)
        oh_key = ohs[:, TILES_REG * R:TILES_REG * (R + KEYS)].rearrange("p (g q k) -> p g q k", g=GROUPS, q=GROUP)
        oh_dst = ohs[:, TILES_REG * (R + KEYS):].rearrange("p (g q k) -> p g q k", g=GROUPS, q=GROUP)
        A_space = sb("A_space", [128, max(NT * AW, XTILES * C)])
        A = A_space[0:R, 0:NT * AW].rearrange("p (c n) -> p c n", c=NT)
        full_dst = oh_key[:, 0:1].rearrange("p g q k -> p (g q k)")
        full_src = sb("full_src", [128, R])
        in_chunk = sb("in_chunk", [128, TILES])

        qk = sb("qk", [R, NT, 2 * C])
        v1 = sb("v1", [R, NT, H, D1])
        gT = sb("gT", [128, KC, NP])
        hT_uT = sb("hT_uT", [128, 2, KC, NP])
        v_left = gT[0:R].rearrange("p k n -> p (k n)")[:, 0:2 * H * D1].rearrange("p (s c) -> p s c", s=2)
        v3 = hT_uT[0:R, :, :, :].rearrange("p a k n -> p (a k n)").bitcast(BF16)[:, 0:NT * H * VP] \
            .rearrange("p (t c j) -> p t c j", t=NT, j=3)
        ss = sb("ss", [R, NT, 2 * H])
        nrm = sb("nrm", [R, NT, 2 * H])
        least = sb("least", [R, 2 * H])
        yT = sb("yT", [128, KC, NP])
        qkT = sb("qkT", [128, 2, H, NP], F16)
        qT, kT = qkT[:, 0], qkT[:, 1]
        work = arena[:, W_WORK:W_OH]
        sq = yT[0:R, :, 0:2 * C]
        split = work[0:R, 0:NT * 4 * C].bitcast(F16).rearrange("p (t a h s d) -> p t a h s d", t=NT, a=2, h=H, s=4)
        P = work[0:R, :].bitcast(F16).rearrange("p (s k j n) -> p s k j n", s=2, k=NT, j=2)
        t_abs = sb("t_abs", [128, H])
        t_inv = sb("t_inv", [128, H])
        t_line = sb("t_line", [128, H, 2])
        t_rest = sb("t_rest", [128, H])
        line = sb("line", [128, 2, 2])
        vrest = sb("vrest", [R, H * D1])
        ysum = sb("ysum", [R, 2, NT, D1])
        rden = sb("rden", [R, 2, NT])
        y = sb("y", [R, NT, C])

        eps1 = sb("eps1", [128, 1])
        hT, uT = hT_uT[:, 0], hT_uT[:, 1]
        bst = sb("bst", [128, KC, 2, 6])
        bmv = sb("bmv", [128, KC, 2])
        bstd = sb("bstd", [128, KC])
        bscale = sb("bscale", [128, KC])
        bshift = sb("bshift", [128, KC])
        btmp = sb("btmp", [128, KC])

        acc = sb("acc", [R, NT, C])
        x2n = y
        x2T = xnT
        prob = sb("prob", [R, NT, NX])
        red = sb("red", [R, NT])
        logit = sb("logit", [R, NT, NX])
        den = sb("den", [R, NT])
        rank1 = sb("rank1", [R, NT, NX])
        tops = sb("tops", [R, 2, NT, NX])
        top1, top2 = tops[:, 0], tops[:, 1]
        rest = sb("rest", [R, NT, NX])
        cw = sb("cw", [R, NT, NX])
        pair = sb("pair", [R, 2, NT, NX])
        wtop = sb("wtop", [R, 2, NT])
        sel = sb("sel", [R, NT, NX], BF16)
        tri = sb("tri", [128, 128], BF16)
        ones16 = sb("ones16", [128, 128], BF16)
        tiles_gt = sb("tiles_gt", [R, NX, NT])
        tiles_e = sb("tiles_e", [R, NX])
        before = sb("before", [R, NX, NX])
        base_e = sb("base_e", [R, NX])
        rank_of = sb("rank_of", [R, 2, NT, NX])
        rank_f = sb("rank_f", [R, 2 * NT])
        rank_i = sb("rank_i", [R, 2 * NT], I32)
        base_of = sb("base_of", [R, 2 * NT, NX])
        base_f = sb("base_f", [R, 2 * NT])
        tile_f = sb("tile_f", [R, 2 * NT])
        tile_i = sb("tile_i", [R, 2 * NT], I32)
        place_i = sb("place_i", [R, 2 * NT], I32)
        oh_place = sb("oh_place", [R, 2 * NT, 128], F16)
        oh_tile = sb("oh_tile", [R, 2 * NT, XTILES], F16)
        row_tile = sb("row_tile", [R, 2 * NT, XTILES], F16)
        token_2 = sb("token_2", [128, XTILES], I32)
        token_i = sb("token_i", [128, XTILES], I32)
        empty = sb("empty", [128, XTILES])
        dest_i = sb("dest_i", [128, XTILES], I32)
        x_all = qkT[:, :, :, :].rearrange("p a h n -> p (a h n)")[:, 0:2 * (XTILES + 2) * C].bitcast(F32)
        y_all = A_space[:, 0:XTILES * C]
        end_e = sb("end_e", [R, NX])
        past = sb("past", [R, XTILES, NX])
        meta = sb("meta", [R, XTILES + 1])
        meta_i = sb("meta_i", [R, XTILES + 1], I32)
        warm = sb("warm", [128, 2])
        x_rows = gT[:, 0, 0:C]
        xT_t = yT[:, 0, 0:KC * 128].rearrange("p (k r) -> p k r", k=KC)
        h_rows = hT[:, 0, 0:HID]
        hT_t = uT[:, 0, 0:MC * 128].rearrange("p (m r) -> p m r", m=MC)
        got = qk[:, :, :].rearrange("p t (j c) -> p t j c", j=2)
        cwT = x_sb[0:NX].rearrange("p t c -> p (t c)")[:, 0:N]

        ident_in, keys_in, weights_in, cst_in, rows_in, cols_in, edges_in = (
            sem(n) for n in ("ident_in", "keys_in", "weights_in", "cst_in", "rows_in", "cols_in", "edges_in"))
        x_in = [sem(f"x_in{t}") for t in range(NT)]
        wqkv_in, wsmall_in = sem("wqkv_in"), sem("wsmall_in")
        fw_in = sem("fw_in")
        x2n_stored, y_scattered, all_scattered, out_done = (
            sem(n) for n in ("x2n_stored", "y_scattered", "all_scattered", "out_done"))
        tile_in = [sem(f"tile_in{g}") for g in range(XTILES)]
        pair_in = [sem(f"pair_in{t}") for t in range(NT)]
        consts_set = sem("consts_set")
        dve_step = sem("dve_step")
        ln_stats, ln_var, ln_std, xn_ready = (sem(n) for n in ("ln_stats", "ln_var", "ln_std", "xn_ready"))
        xT_ps, xT_ready = sem("xT_ps"), sem("xT_ready")
        qkv_ps, qkv_ready = sem("qkv_ps"), sem("qkv_ready")
        sq_ready, ss_ready, nrm_ready, qk_normed, hi_ready, lo_ready, split_ready = (
            sem(n) for n in ("sq_ready", "ss_ready", "nrm_ready", "qk_normed", "hi_ready", "lo_ready", "split_ready"))
        qkT_ps, qkT_ready = sem("qkT_ps"), sem("qkT_ready")
        vsum_ps, vrest_ready = sem("vsum_ps"), sem("vrest_ready")
        pool_step, v3_ready, line_ready, pads_zeroed = (
            sem(n) for n in ("pool_step", "v3_ready", "line_ready", "pads_zeroed"))
        any_ready, flag_max, flag_ready = (sem(n) for n in ("any_ready", "flag_max", "flag_ready"))
        group_free, src_ready, key_ready, dst_ready = (sem(n) for n in ("group_free", "src_ready", "key_ready", "dst_ready"))
        region_ps, region_added = sem("region_ps"), sem("region_added")
        full_ready, full_used, full_ps, full_added = (sem(n) for n in ("full_ready", "full_used", "full_ps", "full_added"))
        adj_zeroed, adj_ready, chunk_set = sem("adj_zeroed"), sem("adj_ready"), sem("chunk_set")
        scores_ready, squares_ready, parts_ready, pv_done, rest_added, head_step, y_ready, yT_ps, yT_ready = (
            sem(n) for n in ("scores_ready", "squares_ready", "parts_ready", "pv_done", "rest_added", "head_step", "y_ready", "yT_ps", "yT_ready"))
        temp_ready, warmed = sem("temp_ready"), sem("warmed")
        agg_ps, agg_ready = sem("agg_ps"), sem("agg_ready")
        lin_ps, lin_ready, bvar_ready, bstd_ready, bn_ready = (
            sem(n) for n in ("lin_ps", "lin_ready", "bvar_ready", "bstd_ready", "bn_ready"))
        mix_ps, mix_added = sem("mix_ps"), sem("mix_added")
        x2n_ready, x2T_ps, x2T_ready = sem("x2n_ready"), sem("x2T_ps"), sem("x2T_ready")
        gate_ps, logits_ready, exp_ready, cw_ready = sem("gate_ps"), sem("logits_ready"), sem("exp_ready"), sem("cw_ready")
        cwT_ps, cwT_ready, bias_ps = sem("cwT_ps"), sem("cwT_ready"), sem("bias_ps")
        sel_ready, rank_ps, place_ready, slots_ps, tokens_ready, dest_ready, meta_ready, bias_added = (
            sem(n) for n in ("sel_ready", "rank_ps", "place_ready", "slots_ps", "tokens_ready", "dest_ready",
                             "meta_ready", "bias_added"))
        tiles_here, x_copied = sem("tiles_here"), sem("x_copied")
        x_turned, xT_copied, up_ps, up_copied, h_turned, gelu_ready, down_ps, y_copied, tile_added = (
            sem(n) for n in ("x_turned", "xT_copied", "up_ps", "up_copied", "h_turned", "gelu_ready", "down_ps",
                             "y_copied", "tile_added"))

        x2n_rows = nc.dram_tensor("x2n_rows", (N, C), F32, kind="Internal").ap()
        y_pairs = nc.dram_tensor("y_pairs", (2 * N + XTILES * 128, C), F32, kind="Internal").ap()
        MIX = (2, 3, 6, 7, 4)

        BIAS = ((4, 0), (4, C), (6, 0), (6, C), (7, 0))

        block = ctx.enter_context(nc.Block())

        @block.sync
        def _(sp):
            for t in range(NT):
                sp.dma_start(x_sb[:, t, :], x[t * R:(t + 1) * R, :]).then_inc(x_in[t], 16)
                if t == 1:
                    sp.dma_start(cst_sb[:, 0:CST_KEY], cst[:, 0:CST_KEY]).then_inc(ident_in, 16)
            sp.dma_start(src_i[:, :], esrc[:, :]).then_inc(edges_in, 16)
            sp.dma_start(dst_i[:, :], edst[:, :]).then_inc(edges_in, 16)
            sp.dma_start(cst_sb[:, CST_KEY:CST_DST], cst[:, CST_KEY:CST_DST]).then_inc(keys_in, 16)
            sp.dma_start(wqkv_sb[:, :, :], wqkvT.rearrange("(k p) n -> p k n", p=128)).then_inc(wqkv_in, 16)
            sp.dma_start(rows_sb[:, :], rows.partition_broadcast(128)).then_inc(rows_in, 16)
            sp.dma_start(w_sb[:, :], ew[:, :]).then_inc(weights_in, 16)
            sp.dma_start(cst_sb[:, CST_DST:CSTS], cst[:, CST_DST:CSTS]).then_inc(cst_in, 16)
            sp.dma_start(cols_sb[:, :], cols[:, :]).then_inc(cols_in, 16)
            for dst, src in ((wproj_sb, wprojT), (gw1_sb, gw1), (gw2_sb, gw2), (gatew_sb, gatew)):
                sp.dma_start(dst[:, :, :], src.rearrange("(k p) n -> p k n", p=128)).then_inc(wsmall_in, 16)
            sp.dma_start(fb2_sb[:, :], fb2[:, :]).then_inc(wsmall_in, 16)
            def expert(e):
                sp.dma_start(arena[:, e * EXPERT:e * EXPERT + KC * HID].rearrange("p (k n) -> p k n", k=KC),
                             fw1[e].rearrange("(k p) n -> p k n", p=128)).then_inc(fw_in, 16)
                sp.dma_start(arena[:, e * EXPERT + KC * HID:(e + 1) * EXPERT].rearrange("p (k n) -> p k n", k=MC),
                             fw2[e].rearrange("(k p) n -> p k n", p=128)).then_inc(fw_in, 16)

            expert(0)
            expert(1)
            sp.wait_ge(adj_ready, 1)
            sp.wait_ge(pv_done, H + 2)
            for e in range(2, NX):
                expert(e)

            for t in range(NT):
                sp.wait_ge(x2n_ready, t + 1)
                sp.dma_start(x2n_rows[t * R:(t + 1) * R, :], x2n[:, t, :]).then_inc(x2n_stored, 16)

            for g in range(XTILES):
                sp.wait_ge(tile_in[g], 16)
                sp.sem_inc(tiles_here, 1)
            sp.sem_inc(tiles_here, 2)

            sp.wait_ge(meta_ready, 1)
            n_tiles = sp.value_load(meta_i[0:1, XTILES:XTILES + 1], min_val=XTILES_MIN, max_val=XTILES)
            sp.wait_ge(y_scattered, n_tiles * 16)
            sp.sem_inc(all_scattered, 1)
            for t in range(NT):
                sp.dma_start(got[:, t].rearrange("p j c -> p (j c)"),
                             y_pairs[2 * t * R:2 * (t + 1) * R, :].rearrange("(p j) c -> p (j c)", j=2)).then_inc(pair_in[t], 16)
            for t in range(NT):
                sp.wait_ge(tile_added, t + 1)
                sp.dma_start(out[t * R:(t + 1) * R, :], acc[:, t, :]).then_inc(out_done, 16)
            sp.wait_ge(out_done, 16 * NT)

        @block.gpsimd
        def _(pool):
            nc.gpsimd.memset(A[:, :, :], 0.0).then_inc(adj_zeroed, 1)
            pool.wait_ge(any_ready, 1)
            nc.gpsimd.partition_all_reduce(any_all[:, :], any_p[:, :], 128, RMAX).then_inc(flag_max, 1)
            steps = [0]

            def then(ins):
                steps[0] += 1
                ins.then_inc(pool_step, 1)
                pool.wait_ge(pool_step, steps[0])

            for t in range(NT):
                pool.wait_ge(qkv_ready, t + 1)
                v = v1[:, t].rearrange("p h d -> p (h d)")
                left = v_left[:, t % 2, :]
                then(nc.gpsimd.tensor_copy(v3[:, t, :, 0], v))
                then(nc.gpsimd.tensor_tensor(left, v, v3[:, t, :, 0], ALU.subtract))
                then(nc.gpsimd.tensor_copy(v3[:, t, :, 1], left))
                nc.gpsimd.tensor_tensor(v3[:, t, :, 2], left, v3[:, t, :, 1], ALU.subtract).then_inc(v3_ready, 1)

            def rows_out(i, s):
                pool.wait_ge(head_step, i * 6 + (3 * s + 3))
                vr = vrest[:, bass.ds(i * (2 * D1) + s * D1, D)]
                nc.gpsimd.tensor_tensor(ysum[:, s, :, 0:D], ysum[:, s, :, 0:D],
                                        vr.unsqueeze(1).to_broadcast([R, NT, D]), ALU.add).then_inc(rest_added, 1)
                pool.wait_ge(rest_added, i * 2 + (s + 1))
                nc.gpsimd.tensor_tensor(y[:, :, bass.ds(i * (2 * D) + s * D, D)], ysum[:, s, :, 0:D],
                                        rden[:, s, :].unsqueeze(2).to_broadcast([R, NT, D]), ALU.mult).then_inc(y_ready, 1)

            def weigh_regions(i, rows):
                for n in range(2 * GROUPS):
                    g = n % GROUPS
                    pool.wait_ge(key_ready, i * (2 * GROUPS) + (n + 1))
                    pool.wait_ge(group_free, i * (2 * GROUPS) + (n + 1))
                    wt = w_sb[:, bass.ds(i * (2 * TILES_REG) + n * GROUP, GROUP)]
                    nc.gpsimd.tensor_tensor(oh_dst[:, g], oh_key[:, g], wt.unsqueeze(2).to_broadcast([128, GROUP, KEYS]),
                                            ALU.mult).then_inc(dst_ready, 1)
                    if g == 0 and rows is not None:
                        rows_out(rows, n // GROUPS)

            pool.wait_ge(weights_in, 16)
            weigh_regions(0, None)
            with pool.Fori(0, H // 2 - 1) as i:
                weigh_regions(i + 1, i)
            for s in range(2):
                rows_out(H // 2 - 1, s)

            pool.wait_ge(tokens_ready, 1)
            pool.wait_ge(x2n_stored, 16 * NT)
            pool.wait_ge(pv_done, H + 2)
            pool.wait_ge(mix_ps, NT)
            for g in range(XTILES):
                nc.gpsimd.indirect_dma_start(
                    out=x_all[:, g * C:(g + 1) * C] if g else x_rows[:, :], out_offset=None, in_=x2n_rows[:, :],
                    in_offset=bass.IndirectOffsetOnAxis(ap=token_i[:, g:g + 1], axis=0)).then_inc(tile_in[g], 16)
            pool.wait_ge(dest_ready, 1)
            pool.wait_ge(meta_ready, 1)
            n_tiles = pool.value_load(meta_i[0:1, XTILES:XTILES + 1], min_val=XTILES_MIN, max_val=XTILES)

            def scatter(g):
                pool.wait_ge(y_copied, g + 2)
                nc.gpsimd.indirect_dma_start(
                    out=y_pairs[:, :], out_offset=bass.IndirectOffsetOnAxis(ap=dest_i[:, g:g + 1], axis=0),
                    in_=y_all[:, g * C:(g + 1) * C], in_offset=None).then_inc(y_scattered, 16)

            for g in range(XTILES):
                if g < XTILES_MIN:
                    scatter(g)
                else:
                    with pool.If(n_tiles > g):
                        scatter(g)

        t_lines = t_line[:, :, :].rearrange("p h j -> p (h j)")

        @block.scalar
        def _(act):
            def row_std(layer, t):
                act.wait_ge(ln_var, layer * NT + t + 1)
                nc.scalar.activation(std[0:R, t:t + 1], mv[0:R, t, 1:2], ACT.Sqrt, bias=eps_c[0:R, :]).then_inc(ln_std, 1)

            act.wait_ge(consts_set, 6)
            nc.scalar.activation(warm[:, 1:2], eps_c[:, :], ACT.Sqrt)
            for t in range(NT):
                row_std(0, t)

            for t in range(NT):
                act.wait_ge(xT_ps, t + 1)
                nc.scalar.copy(xnT[:, :, t * R:(t + 1) * R],
                               ps[:, 2 + t % 2, 0:KC * R].rearrange("p (m r) -> p m r", m=KC)).then_inc(xT_ready, 1)

            for u in range(NT + 4):
                if u < NT:
                    act.wait_ge(qkv_ready, u + 1)
                    nc.scalar.activation(sq[:, u % 2, :], qk[:, u, :], ACT.Square).then_inc(sq_ready, 1)
                if 0 <= u - 1 < NT:
                    act.wait_ge(ss_ready, u)
                    nc.scalar.activation(nrm[:, u - 1, :], ss[:, u - 1, :], ACT.Sqrt, scale=1.0 / SCALE2).then_inc(nrm_ready, 1)
                if 0 <= u - 2 < NT:
                    act.wait_ge(qk_normed, u - 1)
                    for a in range(2):
                        nc.scalar.copy(split[:, u - 2, a, :, 0::3 - a, :][:, :, 0:2],
                                       qk[:, u - 2, a * C:(a + 1) * C].rearrange("p (h d) -> p h d", d=D)
                                       .unsqueeze(2).to_broadcast([R, H, 2, D])).then_inc(hi_ready, 1)
                if 0 <= u - 4:
                    t = u - 4
                    act.wait_ge(qkT_ps, t + 1)
                    for a, buf in ((0, qT), (1, kT)):
                        if t == NT - 1 and a == 1:
                            continue
                        bank = ps16[:, 2 + 2 * (t % 2) + a, 0:H * TS].rearrange("p (h r) -> p h r", h=H)
                        nc.scalar.copy(buf[:, :, t * R:(t + 1) * R], bank[:, :, 0:R]).then_inc(qkT_ready, 1)

            act.wait_ge(line_ready, 1)

            def region_out(i, s):
                act.wait_ge(region_ps, i * 2 + (s + 1))
                nc.scalar.copy(A[:, :, bass.ds(i * (2 * STEP) + s * STEP, REG_NODES)],
                               ps[0:R, s, 0:REG_COLS].rearrange("p (d c) -> p c d", c=NT)).then_inc(region_added, 1)

            def head(prev, this):
                i, s = this
                nc.scalar.copy(line[0:R, s, :],
                               t_lines[0:R, bass.ds(i * 4 + 2 * s, 2)]).then_inc(temp_ready, 1)
                act.wait_ge(temp_ready, i * 2 + (s + 1))
                act.wait_ge(pv_done, i * 2 + (s + 1))
                for kt in range(NT):
                    u = s * NT + kt
                    act.wait_ge(scores_ready, i * (2 * NT) + (u + 1))
                    banks = ps[0:R, 2 + 2 * (u % 2):4 + 2 * (u % 2), 0:HALF]
                    nc.scalar.activation(P[:, s, kt, 0, 0:NP].rearrange("p (a n) -> p a n", a=2), banks, ACT.Square,
                                         bias=line[0:R, s, 1:2], scale=line[0:R, s, 0:1])
                    nc.scalar.activation(banks, banks, ACT.Square,
                                         bias=line[0:R, s, 1:2], scale=line[0:R, s, 0:1]).then_inc(squares_ready, 1)
                    if kt == 0 and prev:
                        region_out(*prev)

            head(None, (0, 0))
            with act.Fori(0, H // 2 - 1) as i:
                head((i, 0), (i, 1))
                head((i, 1), (i + 1, 0))
            last_pair = H // 2 - 1
            head((last_pair, 0), (last_pair, 1))
            region_out(last_pair, 1)

            def y_out(t0, t1):
                for t in range(t0, t1):
                    act.wait_ge(yT_ps, t + 1)
                    nc.scalar.copy(yT[:, :, t * R:(t + 1) * R],
                                   ps[:, 2 + t % 2, 0:KC * R].rearrange("p (m r) -> p m r", m=KC)).then_inc(yT_ready, 1)

            def linear_out(layer):
                for a in range(2):
                    for m in range(KC):
                        act.wait_ge(lin_ps, (layer * 2 + a) * KC + m + 1)
                        if layer == 1 and a == 0 and m == 0:
                            act.wait_ge(bn_ready, 2)
                        b = cols_sb[:, (COL["gb1"] if layer == 0 else COL["gb2"]) + m:][:, 0:1]
                        nc.scalar.activation(hT[:, m, a * HALF:(a + 1) * HALF], ps[:, 4 * m + a, 0:HALF],
                                             ACT.Identity, bias=b).then_inc(lin_ready, 1)

            def bn_std(layer):
                act.wait_ge(bvar_ready, layer + 1)
                nc.scalar.activation(bstd[:, :], bmv[:, :, 1], ACT.Sqrt, bias=eps_c[:, :]).then_inc(bstd_ready, 1)

            act.wait_ge(cols_in, 16)
            linear_out(0)
            y_out(0, 3)
            bn_std(0)
            y_out(3, NT)
            linear_out(1)
            bn_std(1)

            for u in range(NT + 1):
                if u < NT:
                    row_std(1, u)
                if u >= 1:
                    t = u - 1
                    act.wait_ge(x2T_ps, t + 1)
                    nc.scalar.copy(x2T[:, :, t * R:(t + 1) * R],
                                   ps[:, t % 2, 0:KC * R].rearrange("p (m r) -> p m r", m=KC)).then_inc(x2T_ready, 1)

            act.wait_ge(logits_ready, 1)
            nc.scalar.activation(prob[:, :, :], prob[:, :, :], ACT.Exp).then_inc(exp_ready, 1)
            act.wait_ge(cwT_ps, 1)
            nc.scalar.copy(cwT[:, 0:4 * R], ps[0:NX, 7, 0:4 * R]).then_inc(cwT_ready, 1)
            nc.scalar.copy(cwT[:, 4 * R:N], ps[0:NX, 6, 0:R]).then_inc(cwT_ready, 1)

            act.wait_ge(meta_ready, 1)
            n_tiles = act.value_load(meta_i[0:1, XTILES:XTILES + 1], min_val=XTILES_MIN, max_val=XTILES)

            def gelu(g):
                e = act.value_load(meta_i[0:1, bass.ds(g, 1)], min_val=0, max_val=NX - 1)
                nc.scalar.activation(warm[:, 0:1], eps_c[:, :], ACT.Gelu).then_inc(warmed, 1)
                act.wait_ge(warmed, g + 1)
                act.wait_ge(h_turned, g + 1)
                for m in range(MC):
                    b = cols_sb[:, bass.ds(e * MC + (COL_FB1 + m), 1)]
                    nc.scalar.activation(hT_t[:, m, :], ps[:, 1, m * 128:(m + 1) * 128], ACT.Gelu,
                                         bias=b).then_inc(gelu_ready, 1)

            with act.Fori(0, n_tiles - 1) as g:
                gelu(g)
            gelu(n_tiles - 1)

        @block.vector
        def _(dve):
            steps = [0]

            def then(ins):
                steps[0] += 1
                ins.then_inc(dve_step, 1)
                dve.wait_ge(dve_step, steps[0])

            def mark(ins):
                steps[0] += 1
                ins.then_inc(dve_step, 1)
                return steps[0]

            def seen(step):
                dve.wait_ge(dve_step, step)

            nc.vector.memset(eps_c[:, :], LN_EPS).then_inc(consts_set, 1)
            nc.vector.memset(zeros[:, :], 0.0).then_inc(consts_set, 1)
            nc.vector.memset(ones_r[:, :], 1.0).then_inc(consts_set, 1)
            for buf in (xnT, qT):
                nc.vector.memset(buf[:, :, N:NP], 0.0).then_inc(consts_set, 1)
            nc.vector.memset(v1[:, :, :, D:D1].rearrange("p t h o -> p t (h o)"), 1.0).then_inc(consts_set, 1)
            dve.wait_ge(consts_set, 6)

            def row_norm(src, dst, ready, layer, arrive, arrived):
                for u in range(NT + 3):
                    t = u - 3
                    if u < NT:
                        arrive(u)
                    if t >= 0:
                        dve.wait_ge(ln_std, layer * NT + t + 1)
                        inverse = mark(nc.vector.reciprocal(rstd[0:R, t:t + 1], std[0:R, t:t + 1]))
                    if u < NT:
                        arrived(u)
                        nc.vector.bn_stats(stats[0:R, u, :], src[:, u, :]).then_inc(ln_stats, 1)
                    if t >= 0:
                        seen(inverse)
                        nc.vector.tensor_scalar(dst[:, t, :], src[:, t, :], mv[0:R, t, 0:1], rstd[0:R, t:t + 1],
                                                ALU.subtract, ALU.mult).then_inc(ready, 1)
                    if 0 <= u - 1 < NT:
                        dve.wait_ge(ln_stats, layer * NT + u)
                        nc.vector.bn_aggr(mv[0:R, u - 1, :], stats[0:R, u - 1, :]).then_inc(ln_var, 1)

            row_norm(x_sb, xn, xn_ready, 0, lambda t: None, lambda t: dve.wait_ge(x_in[t], 16))
            nc.vector.memset(least[:, 0:H], 1e-12 / SCALE2)
            nc.vector.memset(least[:, H:2 * H], 1e-12 / SCALE)

            dve.wait_ge(ident_in, 16)
            nc.vector.tensor_copy(ident16[:, :], ident)
            dve.wait_ge(edges_in, 32)
            dve.wait_ge(keys_in, 16)
            nc.vector.tensor_copy(srcf[:, :], src_i[:, :])
            then(nc.vector.tensor_copy(dstf[:, :], dst_i[:, :]))
            then(nc.vector.tensor_scalar(chunk[:, :], srcf[:, :], float(R), None, ALU.is_ge))
            for c in range(2, NT):
                then(nc.vector.scalar_tensor_tensor(chunk[:, :], srcf[:, :], float(c * R), chunk[:, :],
                                                    ALU.is_ge, ALU.add))
            nc.vector.scalar_tensor_tensor(srow[:, :], chunk[:, :], -float(R), srcf[:, :], ALU.mult, ALU.add)
            then(nc.vector.scalar_tensor_tensor(key[:, :], dstf[:, :], float(NT), cst_sb[:, CST_KEY:CST_KEY + TILES],
                                                ALU.mult, ALU.add))
            then(nc.vector.tensor_tensor(key[:, :], key[:, :], chunk[:, :], ALU.add))
            then(nc.vector.tensor_scalar(out_lo[:, :], key[:, :], 0.0, None, ALU.is_lt))

            then(nc.vector.scalar_tensor_tensor(out_win[:, :], key[:, :], float(KEYS), out_lo[:, :], ALU.is_ge, ALU.add))
            nc.vector.reduce_max(any_p[:, :], out_win[:, 0:REAL_TILES], AX.X).then_inc(any_ready, 1)

            def group_tiles(i, s, g):
                return bass.ds(i * (2 * TILES_REG) + (s * GROUPS + g) * GROUP, GROUP)

            def key_rows(i, s, g):
                dve.wait_ge(group_free, i * (2 * GROUPS) + (s * GROUPS + g + 1))
                nc.vector.tensor_tensor(oh_key[:, g], iota[:, 0:KEYS].unsqueeze(1).to_broadcast([128, GROUP, KEYS]),
                                        key[:, group_tiles(i, s, g)].unsqueeze(2).to_broadcast([128, GROUP, KEYS]),
                                        ALU.is_equal).then_inc(key_ready, 1)

            def src_rows(i, s, g):
                nc.vector.tensor_tensor(oh_src[:, g], iota[:, 0:R].unsqueeze(1).to_broadcast([128, GROUP, R]),
                                        srow[:, group_tiles(i, s, g)].unsqueeze(2).to_broadcast([128, GROUP, R]),
                                        ALU.is_equal).then_inc(src_ready, 1)

            dve.wait_ge(rows_in, 16)
            temps = rows_sb[:, ROW_TEMP:ROW_TEMP + H]
            then(nc.vector.scalar_tensor_tensor(t_abs[:, :], temps, -1.0, temps, ALU.mult, ALU.max))
            then(nc.vector.tensor_scalar(t_abs[:, :], t_abs[:, :], 1.0, None, ALU.add))
            then(nc.vector.reciprocal(t_inv[:, :], t_abs[:, :]))
            nc.vector.tensor_tensor(t_line[:, :, 0], temps, t_inv[:, :], ALU.mult)
            then(nc.vector.tensor_tensor(t_rest[:, :], t_inv[:, :], t_inv[:, :], ALU.mult))
            nc.vector.tensor_scalar(t_line[:, :, 1], t_inv[:, :], SHIFT, None, ALU.mult).then_inc(line_ready, 1)
            then(nc.vector.tensor_scalar(t_rest[:, :], t_rest[:, :], REST, None, ALU.mult))
            key_rows(0, 0, 0)

            for u in range(NT + 3):
                if u < NT:
                    dve.wait_ge(qkv_ps, u + 1)
                    nc.vector.tensor_tensor(qk[:, u, :], ps[0:R, 4 + 2 * (u % 2), 0:512],
                                            rows_sb[0:R, ROW_BQKV:ROW_BQKV + 512], ALU.add)
                    nc.vector.tensor_tensor(v1[:, u, :, 0:D],
                                            ps[0:R, 5 + 2 * (u % 2), 0:256].rearrange("p (h d) -> p h d", d=D),
                                            rows_sb[0:R, ROW_BQKV + 512:ROW_BQKV + 768].rearrange("p (h d) -> p h d", d=D),
                                            ALU.add).then_inc(qkv_ready, 1)
                if u == 0:
                    src_rows(0, 0, 0)
                if u == 1:
                    key_rows(0, 0, 1)
                if u == 2:
                    src_rows(0, 0, 1)
                if 0 <= u - 1 < NT:
                    dve.wait_ge(sq_ready, u)
                    nc.vector.tensor_reduce(ss[:, u - 1, :], sq[:, (u - 1) % 2, :].rearrange("p (h d) -> p h d", d=D),
                                            AX.X, ALU.add).then_inc(ss_ready, 1)
                if 0 <= u - 2 < NT:
                    t = u - 2
                    dve.wait_ge(nrm_ready, t + 1)
                    then(nc.vector.tensor_tensor(nrm[:, t, :], nrm[:, t, :], least[:, :], ALU.max))
                    then(nc.vector.reciprocal(nrm[:, t, :], nrm[:, t, :]))
                    rows3 = qk[:, t, :].rearrange("p (h d) -> p h d", d=D)
                    nc.vector.tensor_tensor(rows3, rows3, nrm[:, t, :].unsqueeze(2).to_broadcast([R, 2 * H, D]),
                                            ALU.mult).then_inc(qk_normed, 1)
                if 0 <= u - 3:
                    t = u - 3
                    dve.wait_ge(hi_ready, 2 * (t + 1))
                    parts = split[:, t].rearrange("p a h s d -> p (a h) s d")
                    then(nc.vector.tensor_tensor(parts[:, :, 1, :], qk[:, t, :].rearrange("p (a d) -> p a d", d=D),
                                                 parts[:, :, 0, :], ALU.subtract))
                    nc.vector.tensor_copy(split[:, t, 0, :, 2, :], split[:, t, 0, :, 1, :])
                    nc.vector.tensor_copy(split[:, t, 1, :, 3, :], split[:, t, 1, :, 1, :]).then_inc(split_ready, 1)
            dve.wait_ge(flag_max, 1)
            nc.vector.tensor_copy(flag[:, :], any_all[:, :]).then_inc(flag_ready, 1)
            dve.wait_ge(weights_in, 16)
            nc.vector.tensor_tensor(w_out[:, :], out_win[:, :], w_sb[:, :], ALU.mult)
            dve.wait_ge(cst_in, 16)
            nc.vector.tensor_copy(tri[:, :], cst_sb[:, CST_TRI:CST_TRI + 128])
            nc.vector.memset(ones16[:, :], 1.0)
            nc.vector.tensor_scalar(eps1[:, :], rows_sb[:, ROW_EPS:ROW_EPS + 1], 1.0, None, ALU.add)
            dve.wait_ge(adj_zeroed, 1)
            dve.wait_ge(vsum_ps, 1)
            nc.vector.tensor_tensor(vrest[:, :].rearrange("p (h d) -> p h d", h=H),
                                    ps[0:R, 6, 0:H * D1].rearrange("p (h d) -> p h d", h=H),
                                    t_rest[0:R, :].unsqueeze(2).to_broadcast([R, H, D1]), ALU.mult).then_inc(vrest_ready, 1)
            dve.wait_ge(qkT_ps, NT)
            nc.vector.tensor_copy(kT[:, :, (NT - 1) * R:NT * R],
                                  ps16[:, 3 + 2 * ((NT - 1) % 2), 0:H * TS].rearrange("p (h r) -> p h r", h=H)[:, :, 0:R]
                                  ).then_inc(qkT_ready, 1)
            nc.vector.memset(P[:, :, :, :, NP:PW].rearrange("p s k j n -> p (s k j) n"), 0.0).then_inc(pads_zeroed, 1)
            key_rows(0, 0, 2)
            src_rows(0, 0, 2)
            dve.wait_ge(vrest_ready, 1)

            def rows_sum(i, s):
                dve.wait_ge(pv_done, i * 2 + (s + 3))
                dve.wait_ge(y_ready, i * 2 + (s + 1))
                nc.vector.tensor_reduce(ysum[:, s], ps[0:R, 6 + s, 0:NT * VP].rearrange("p (t d j) -> p t d j", t=NT, j=3),
                                        AX.X, ALU.add).then_inc(head_step, 1)

            def rows_weight(i, s):
                dve.wait_ge(head_step, i * 6 + (3 * s + 1))
                nc.vector.tensor_tensor(rden[:, s, :], ysum[:, s, :, D],
                                        vrest[:, bass.ds(i * (2 * D1) + (s * D1 + D), 1)].to_broadcast([R, NT]),
                                        ALU.add).then_inc(head_step, 1)

            def rows_inverse(i, s):
                dve.wait_ge(head_step, i * 6 + (3 * s + 2))
                nc.vector.reciprocal(rden[:, s, :], rden[:, s, :]).then_inc(head_step, 1)

            def low(i, s, kt):
                u = s * NT + kt
                dve.wait_ge(squares_ready, i * (2 * NT) + (u + 1))
                nc.vector.tensor_tensor(P[:, s, kt, 1, 0:NP].rearrange("p (a n) -> p a n", a=2),
                                        ps[0:R, 2 + 2 * (u % 2):4 + 2 * (u % 2), 0:HALF],
                                        P[:, s, kt, 0, 0:NP].rearrange("p (a n) -> p a n", a=2),
                                        ALU.subtract).then_inc(parts_ready, 1)

            def head(prev, this, following):
                def at(where, step, *args):
                    if where is not None:
                        step(*where, *args)

                at(following, key_rows, 0)
                low(*this, 1)
                at(prev, rows_sum)
                at(following, src_rows, 0)
                at(prev, rows_weight)
                low(*this, 2)
                at(prev, rows_inverse)
                at(following, key_rows, 1)
                low(*this, 3)
                at(following, src_rows, 1)
                if following is not None:
                    low(*this, 4)
                    key_rows(*following, 2)
                    src_rows(*following, 2)
                    low(*following, 0)

            anyf = dve.value_load(flag[0:1, 0:1], min_val=0, max_val=1)
            low(0, 0, 0)
            head(None, (0, 0), (0, 1))
            with dve.Fori(0, H // 2 - 1) as i:
                head((i, 0), (i, 1), (i + 1, 0))
                head((i, 1), (i + 1, 0), (i + 1, 1))
            last = H // 2 - 1
            head((last, 0), (last, 1), None)
            dve.wait_ge(region_added, REGIONS + 2)
            with dve.If(anyf > 0):
                dve.sem_inc(full_used, 1)
                for c in range(NT):
                    nc.vector.tensor_scalar(in_chunk[:, :], chunk[:, :], float(c), None,
                                            ALU.is_equal).then_inc(chunk_set, 1)
                    dve.wait_ge(chunk_set, 2 * c + 1)
                    nc.vector.tensor_tensor(in_chunk[:, :], in_chunk[:, :], w_out[:, :], ALU.mult).then_inc(chunk_set, 1)
                    dve.wait_ge(chunk_set, 2 * c + 2)
                    with dve.Fori(0, TILES) as t:
                        dve.wait_ge(full_used, t + (c * TILES + 1))
                        nc.vector.tensor_scalar(full_dst[:, 0:N], cst_sb[:, CST_DST:CST_DST + N],
                                                dstf[:, bass.ds(t, 1)], None, ALU.is_equal)
                        nc.vector.tensor_scalar(full_src[:, :], iota[:, 0:R], srow[:, bass.ds(t, 1)],
                                                in_chunk[:, bass.ds(t, 1)], ALU.is_equal,
                                                ALU.mult).then_inc(full_ready, 1)
                    dve.wait_ge(full_ps, c + 1)
                    for a, n0, n1 in ((0, 0, HALF), (1, HALF, N)):
                        nc.vector.tensor_tensor(A[:, c, BEFORE + n0:BEFORE + n1], A[:, c, BEFORE + n0:BEFORE + n1],
                                                ps[0:R, a, 0:n1 - n0], ALU.add).then_inc(full_added, 1)
            dve.sem_inc(adj_ready, 1)
            low(last, 1, NT - 1)

            def aggregate():
                for a in range(2):
                    for m in range(KC):
                        dve.wait_ge(agg_ps, a * KC + m + 1)
                        nc.vector.scalar_tensor_tensor(gT[:, m, a * HALF:(a + 1) * HALF],
                                                       xnT[:, m, a * HALF:(a + 1) * HALF], eps1[:, :],
                                                       ps[:, 4 * m + a, 0:HALF], ALU.mult, ALU.add).then_inc(agg_ready, 1)

            def batch_norm(layer, dst, gcol, becol):
                for a in range(2):
                    for m in range(KC):
                        dve.wait_ge(lin_ready, (layer * 2 + a) * KC + m + 1)
                        last = nc.vector.bn_stats(bst[:, m, a, :], hT[:, m, a * HALF:min((a + 1) * HALF, N)])
                then(last)
                for m in range(KC):
                    last = nc.vector.bn_aggr(bmv[:, m, :], bst[:, m, :, :])
                last.then_inc(bvar_ready, 1)
                dve.wait_ge(bstd_ready, layer + 1)
                then(nc.vector.reciprocal(bscale[:, :], bstd[:, :]))
                then(nc.vector.tensor_tensor(bscale[:, :], bscale[:, :], cols_sb[:, gcol:gcol + KC], ALU.mult))
                then(nc.vector.tensor_tensor(btmp[:, :], bmv[:, :, 0], bscale[:, :], ALU.mult))
                then(nc.vector.tensor_tensor(bshift[:, :], cols_sb[:, becol:becol + KC], btmp[:, :], ALU.subtract))
                for a in range(2):
                    for m in range(KC):
                        last = nc.vector.tensor_scalar(dst[:, m, a * HALF:(a + 1) * HALF], hT[:, m, a * HALF:(a + 1) * HALF],
                                                       bscale[:, m:m + 1], bshift[:, m:m + 1], ALU.mult, ALU.add)
                    last.then_inc(bn_ready, 1)

            dve.wait_ge(cols_in, 16)
            for step in (rows_sum, rows_weight, rows_inverse):
                step(last, 1)
            aggregate()
            for t in range(NT):
                last = nc.vector.tensor_tensor(acc[:, t, :], x_sb[:, t, :], rows_sb[0:R, ROW_BPROJ:ROW_BPROJ + C], ALU.add)
            then(last)
            batch_norm(0, uT, COL["gg1"], COL["gbe1"])
            batch_norm(1, gT, COL["gg2"], COL["gbe2"])
            def add_branches(t):
                dve.wait_ge(mix_ps, t + 1)
                nc.vector.tensor_tensor(acc[:, t, :], acc[:, t, :], ps[0:R, MIX[t], 0:C],
                                        ALU.add).then_inc(mix_added, 1)

            row_norm(acc, x2n, x2n_ready, 1, add_branches, lambda t: dve.wait_ge(mix_added, t + 1))

            def per_row(op_out, a, b, op):
                return nc.vector.tensor_tensor(op_out, a, b[:, :].unsqueeze(2).to_broadcast([R, NT, NX]), op)

            rank = cst_sb[0:R, CST_RANK:CST_RANK + NX].unsqueeze(1).to_broadcast([R, NT, NX])
            dve.wait_ge(gate_ps, 1)
            then(nc.vector.tensor_tensor(logit[:, :, :], ps[0:R, 7, 0:NT * NX].rearrange("p (t e) -> p t e", t=NT),
                                         rows_sb[0:R, ROW_GB:ROW_GB + NX].unsqueeze(1).to_broadcast([R, NT, NX]),
                                         ALU.add))
            then(nc.vector.tensor_reduce(red[:, :], logit[:, :, :], AX.X, ALU.max))
            step = mark(per_row(rank1[:, :, :], logit[:, :, :], red, ALU.is_equal))
            per_row(prob[:, :, :], logit[:, :, :], red, ALU.subtract).then_inc(logits_ready, 1)
            seen(step)
            then(nc.vector.tensor_tensor(rank1[:, :, :], rank1[:, :, :], rank, ALU.mult))
            then(nc.vector.tensor_reduce(red[:, :], rank1[:, :, :], AX.X, ALU.max))
            then(per_row(top1, rank1[:, :, :], red, ALU.is_equal))
            then(nc.vector.scalar_tensor_tensor(rest[:, :, :], top1, -FAR, logit[:, :, :], ALU.mult, ALU.add))
            step = mark(nc.vector.tensor_reduce(red[:, :], rest[:, :, :], AX.X, ALU.max))
            dve.wait_ge(exp_ready, 1)
            total = mark(nc.vector.tensor_reduce(den[:, :], prob[:, :, :], AX.X, ALU.add))
            seen(step)
            step = mark(per_row(rank1[:, :, :], rest[:, :, :], red, ALU.is_equal))
            seen(total)
            inverse = mark(nc.vector.reciprocal(den[:, :], den[:, :]))
            seen(step)
            step = mark(nc.vector.tensor_tensor(rank1[:, :, :], rank1[:, :, :], rank, ALU.mult))
            seen(inverse)
            weights = mark(per_row(prob[:, :, :], prob[:, :, :], den, ALU.mult))
            seen(step)
            then(nc.vector.tensor_reduce(red[:, :], rank1[:, :, :], AX.X, ALU.max))
            then(per_row(top2, rank1[:, :, :], red, ALU.is_equal))
            nc.vector.tensor_tensor(sel[:, :, :], top1, top2, ALU.add).then_inc(sel_ready, 1)

            tops_jt = tops[:, :, :, :].rearrange("p j t e -> p j (t e)")
            tops_rows = tops[:, :, :, :].rearrange("p j t e -> p (j t) e")

            def per_choice(dst, of_te):
                return nc.vector.tensor_tensor(dst[:, :, :, :].rearrange("p j t e -> p j (t e)"), tops_jt,
                                               of_te.unsqueeze(1).to_broadcast([R, 2, NT * NX]), ALU.mult)

            seen(weights)
            then(per_choice(pair, prob[:, :, :].rearrange("p t e -> p (t e)")))
            nc.vector.tensor_tensor(cw[:, :, :], pair[:, 0], pair[:, 1], ALU.add).then_inc(cw_ready, 1)
            nc.vector.tensor_reduce(wtop[:, :, :], pair[:, :, :, :], AX.X, ALU.add)

            dve.wait_ge(rank_ps, 1)
            step = mark(nc.vector.tensor_tensor(tiles_gt[:, :, :],
                                                ps[0:R, 5, NT * NX:(NT + 1) * NX].unsqueeze(2).to_broadcast([R, NX, NT]),
                                                cst_sb[0:R, CST_THR:CST_THR + NT].unsqueeze(1).to_broadcast([R, NX, NT]),
                                                ALU.is_gt))
            ranks = mark(per_choice(rank_of, ps[0:R, 5, 0:NT * NX]))
            seen(step)
            step = mark(nc.vector.tensor_reduce(tiles_e[:, :], tiles_gt[:, :, :], AX.X, ALU.add))
            seen(ranks)
            ranks = mark(nc.vector.tensor_reduce(rank_f[:, :], rank_of[:, :, :, :].rearrange("p j t e -> p (j t) e"),
                                                 AX.X, ALU.add))
            seen(step)
            step = mark(nc.vector.tensor_tensor(before[:, :, :], tiles_e[:, :].unsqueeze(1).to_broadcast([R, NX, NX]),
                                                cst_sb[0:R, CST_LT:CST_LT + NX * NX].rearrange("p (a b) -> p a b", a=NX),
                                                ALU.mult))
            seen(ranks)
            ranks = mark(nc.vector.tensor_copy(rank_i[:, :], rank_f[:, :]))
            seen(step)
            step = mark(nc.vector.tensor_reduce(base_e[:, :], before[:, :, :], AX.X, ALU.add))
            seen(ranks)
            nc.vector.tensor_scalar(tile_i[:, :], rank_i[:, :], 7, None, ALU.logical_shift_right)
            places = mark(nc.vector.tensor_scalar(place_i[:, :], rank_i[:, :], 127, None, ALU.bitwise_and))
            seen(step)
            step = mark(nc.vector.tensor_tensor(base_of[:, :, :], tops_rows,
                                                base_e[:, :].unsqueeze(1).to_broadcast([R, 2 * NT, NX]), ALU.mult))
            seen(places)
            nc.vector.tensor_tensor(oh_place[:, :, :], iota[0:R, :].unsqueeze(1).to_broadcast([R, 2 * NT, 128]),
                                    place_i[:, :].unsqueeze(2).to_broadcast([R, 2 * NT, 128]), ALU.is_equal)
            seen(step)
            then(nc.vector.tensor_reduce(base_f[:, :], base_of[:, :, :], AX.X, ALU.add))
            then(nc.vector.tensor_tensor(tile_f[:, :], tile_i[:, :], base_f[:, :], ALU.add))
            then(nc.vector.tensor_tensor(oh_tile[:, :, :],
                                         iota[0:R, 0:XTILES].unsqueeze(1).to_broadcast([R, 2 * NT, XTILES]),
                                         tile_f[:, :].unsqueeze(2).to_broadcast([R, 2 * NT, XTILES]), ALU.is_equal))
            nc.vector.tensor_tensor(row_tile[:, :, :], oh_tile[:, :, :],
                                    cst_sb[0:R, CST_ROW:CST_ROW + 2 * NT].unsqueeze(2).to_broadcast([R, 2 * NT, XTILES]),
                                    ALU.mult).then_inc(place_ready, 1)
            then(nc.vector.tensor_tensor(end_e[:, :], base_e[:, :], tiles_e[:, :], ALU.add))
            then(nc.vector.tensor_tensor(past[:, :, :],
                                         cst_sb[0:R, CST_G:CST_G + XTILES].unsqueeze(2).to_broadcast([R, XTILES, NX]),
                                         end_e[:, :].unsqueeze(1).to_broadcast([R, XTILES, NX]), ALU.is_ge))
            nc.vector.tensor_reduce(meta[:, 0:XTILES], past[:, :, :], AX.X, ALU.add)
            then(nc.vector.tensor_copy(meta[:, XTILES:XTILES + 1], end_e[:, NX - 1:NX]))
            nc.vector.tensor_copy(meta_i[:, :], meta[:, :]).then_inc(meta_ready, 1)
            dve.wait_ge(slots_ps, 1)
            then(nc.vector.tensor_scalar(token_2[:, :], ps[:, 0, 0:XTILES], -1.0, 0.0, ALU.add, ALU.max))
            nc.vector.tensor_scalar(token_i[:, :], token_2[:, :], 1, None, ALU.logical_shift_right).then_inc(tokens_ready, 1)
            then(nc.vector.scalar_tensor_tensor(empty[:, :], ps[:, 0, 0:XTILES], 0.0,
                                                cst_sb[:, CST_EMPTY:CST_EMPTY + XTILES], ALU.is_equal, ALU.mult))
            nc.vector.scalar_tensor_tensor(dest_i[:, :], ps[:, 0, 0:XTILES], -1.0, empty[:, :],
                                           ALU.add, ALU.add).then_inc(dest_ready, 1)
            dve.wait_ge(meta_ready, 1)
            n_tiles = dve.value_load(meta_i[0:1, XTILES:XTILES + 1], min_val=XTILES_MIN, max_val=XTILES)

            def copy_xT(g):
                dve.wait_ge(x_turned, g + 2)
                nc.vector.tensor_copy(xT_t[:, :, :],
                                      ps[:, 2, 0:KC * 128].rearrange("p (m r) -> p m r", m=KC)).then_inc(xT_copied, 1)

            def copy_up(g):
                dve.wait_ge(up_ps, g + 1)
                nc.vector.tensor_copy(h_rows[:, :], ps[:, 0, 0:HID]).then_inc(up_copied, 1)

            def copy_y(g):
                dve.wait_ge(down_ps, g + 1)
                nc.vector.tensor_copy(y_all[:, bass.ds(g * C, C)], ps[:, 3, 0:C]).then_inc(y_copied, 1)

            def copy_x(g):
                dve.wait_ge(tiles_here, g + 1)
                dve.wait_ge(x_turned, g + 1)
                nc.vector.tensor_copy(x_rows[:, :], x_all[:, bass.ds(g * C, C)]).then_inc(x_copied, 1)

            copy_xT(0)
            copy_x(1)
            dve.wait_ge(bias_ps, NT)
            for t in range(NT):
                nc.vector.tensor_tensor(acc[:, t, :], acc[:, t, :], ps[0:R, BIAS[t][0], BIAS[t][1]:BIAS[t][1] + C],
                                        ALU.add).then_inc(bias_added, 1)
            copy_up(0)
            copy_xT(1)
            copy_x(2)
            with dve.Fori(0, n_tiles - 1) as g:
                copy_up(g + 1)
                copy_xT(g + 2)
                copy_x(g + 3)
                copy_y(g)
            copy_y(n_tiles - 1)

            for u in range(NT + 1):
                if u < NT:
                    dve.wait_ge(pair_in[u], 16)
                    if u == 0:
                        dve.wait_ge(bias_added, NT)
                    first = mark(nc.vector.scalar_tensor_tensor(acc[:, u, :], got[:, u, 0, :], wtop[:, 0, u:u + 1],
                                                                acc[:, u, :], ALU.mult, ALU.add))
                if u >= 1:
                    t = u - 1
                    seen(first_of_tile)
                    nc.vector.scalar_tensor_tensor(acc[:, t, :], got[:, t, 1, :], wtop[:, 1, t:t + 1], acc[:, t, :],
                                                   ALU.mult, ALU.add).then_inc(tile_added, 1)
                first_of_tile = first

        @block.tensor
        def _(pe):
            pe.sem_inc(group_free, GROUPS)
            pe.sem_inc(region_added, 2)
            pe.sem_inc(parts_ready, 2)
            pe.sem_inc(pv_done, 2)
            pe.sem_inc(y_ready, 2)
            pe.sem_inc(x_turned, 1)
            pe.sem_inc(y_copied, 1)
            pe.wait_ge(consts_set, 6)
            pe.wait_ge(ident_in, 16)

            for t in range(NT):
                pe.wait_ge(xn_ready, t + 1)
                if t >= 2:
                    pe.wait_ge(xT_ready, t - 1)
                for m in range(KC):
                    last = nc.tensor.transpose(ps[:, 2 + t % 2, m * R:(m + 1) * R],
                                               xn[:, t, m * 128:(m + 1) * 128], ident[0:R, 0:R])
                last.then_inc(xT_ps, 1)

            pe.wait_ge(wqkv_in, 16)

            def project(t):
                pe.wait_ge(xT_ready, t + 1)
                if t >= 2:
                    pe.wait_ge(qkv_ready, t - 1)
                for a, n0, n1 in ((0, 0, 512), (1, 512, 768)):
                    for k in range(KC):
                        last = nc.tensor.matmul(ps[0:R, 4 + 2 * (t % 2) + a, 0:n1 - n0],
                                                xnT[:, k, t * R:(t + 1) * R], wqkv_sb[:, k, n0:n1],
                                                start=(k == 0), stop=(k == KC - 1))
                last.then_inc(qkv_ps, 1)

            for t in range(NT):
                project(t)

            def edge_group(i, r, g):
                n = r * GROUPS + g
                pe.wait_ge(src_ready, i * (2 * GROUPS) + (n + 1))
                pe.wait_ge(dst_ready, i * (2 * GROUPS) + (n + 1))
                for q in range(GROUP):
                    at = TILE_OFF[g * GROUP + q] * NT
                    last = nc.tensor.matmul(ps[0:R, r, at:at + KEYS], oh_src[:, g, q, :], oh_dst[:, g, q, :],
                                            start=False, stop=False, skip_group_check=True)
                last.then_inc(group_free, 1)

            def open_region(i, s):
                pe.wait_ge(region_added, i * 2 + (s + 1))
                nc.tensor.matmul(ps[0:R, s, 0:REG_COLS], zeros[:, 0:R], zeros[:, 0:REG_COLS],
                                 start=True, stop=False, skip_group_check=True)
                edge_group(i, s, 0)

            for t in range(NT):
                if t == 1:
                    pe.wait_ge(qkv_ready, NT)
                    for c in range(NT):
                        last = nc.tensor.matmul(ps[0:R, 6, 0:H * D1], ones_r[0:R, :],
                                                v1[:, c].rearrange("p h d -> p (h d)"), start=(c == 0), stop=(c == NT - 1))
                    last.then_inc(vsum_ps, 1)
                if t == NT - 1:
                    open_region(0, 0)
                pe.wait_ge(split_ready, t + 1)
                if t >= 2:
                    pe.wait_ge(qkT_ready, 2 * (t - 1))
                for a in range(2):
                    for h in range(H):
                        last = nc.tensor.transpose(ps16[:, 2 + 2 * (t % 2) + a, h * TS:h * TS + R],
                                                   split[:, t, a, h].rearrange("p s d -> p (s d)"), ident16[0:R, 0:R])
                last.then_inc(qkT_ps, 1)
            pe.wait_ge(flag_ready, 1)
            anyf = pe.value_load(flag[0:1, 0:1], min_val=0, max_val=1)
            pe.wait_ge(qkT_ready, 2 * NT)

            def scores(i, s, kt):
                u = s * NT + kt
                pe.wait_ge(parts_ready, i * (2 * NT) + (u + 1))
                head = i * 2 + s
                for a in range(2):
                    last = nc.tensor.matmul(ps[0:R, 2 + 2 * (u % 2) + a, 0:HALF],
                                            kT_flat[:, bass.ds(head * NP + kt * R, R)],
                                            qT_flat[:, bass.ds(head * NP + a * HALF, HALF)], start=True, stop=True)
                last.then_inc(scores_ready, 1)

            def weigh(i, s):
                pe.wait_ge(parts_ready, i * (2 * NT) + ((s + 1) * NT + 2))
                for qt in range(NT):
                    for kt in range(NT):
                        for j in range(2):
                            last = nc.tensor.matmul(ps[:, 6 + s, qt * VP:(qt + 1) * VP],
                                                    P[:, s, kt, j, qt * R:qt * R + 128],
                                                    v3_flat[:, bass.ds(kt * (H * VP) + (i * 2 + s) * VP, VP)],
                                                    start=(kt == 0 and j == 0), stop=(kt == NT - 1 and j == 1))
                last.then_inc(pv_done, 1)

            kT_flat = kT[:, :, :].rearrange("p h n -> p (h n)")
            qT_flat = qT[:, :, :].rearrange("p h n -> p (h n)")
            v3_flat = v3[:, :, :, :].rearrange("p t c j -> p (t c j)")

            def head(this, following):
                i, s = this
                scores(i, s, 2)
                scores(i, s, 3)
                edge_group(i, s, 1)
                scores(i, s, 4)
                edge_group(i, s, 2)
                pe.wait_ge(region_added, i * 2 + (s + 2))
                nc.tensor.matmul(ps[0:R, s, 0:SHARED * NT].rearrange("p (d c) -> p d c", c=NT), ident[0:R, 0:R],
                                 A[:, :, bass.ds(i * (2 * STEP) + s * STEP, SHARED)].rearrange("p c d -> p d c"),
                                 start=False, stop=False, skip_group_check=True)
                nc.tensor.matmul(ps[0:R, s, 0:REG_COLS], zeros[:, 0:R], zeros[:, 0:REG_COLS],
                                 start=False, stop=True, skip_group_check=True).then_inc(region_ps, 1)
                if following:
                    scores(*following, 0)
                    open_region(*following)
                    scores(*following, 1)
                    weigh(i, s)

            scores(0, 0, 0)
            scores(0, 0, 1)
            pe.wait_ge(vrest_ready, 1)
            pe.wait_ge(v3_ready, NT)
            pe.wait_ge(pads_zeroed, 1)
            head((0, 0), (0, 1))
            with pe.Fori(0, H // 2 - 1) as i:
                head((i, 1), (i + 1, 0))
                head((i + 1, 0), (i + 1, 1))
            head((H // 2 - 1, 1), None)

            pe.wait_ge(region_added, REGIONS + 2)
            with pe.If(anyf > 0):
                for c in range(NT):
                    if c:
                        pe.wait_ge(full_added, 2 * c)
                    for a in range(2):
                        nc.tensor.matmul(ps[0:R, a, 0:HALF], zeros[:, 0:R], zeros[:, 0:HALF],
                                         start=True, stop=False, skip_group_check=True)
                    with pe.Fori(0, TILES) as t:
                        pe.wait_ge(full_ready, t + (c * TILES + 1))
                        for a, n0, n1 in ((0, 0, HALF), (1, HALF, N)):
                            last = nc.tensor.matmul(ps[0:R, a, 0:n1 - n0], full_src[:, :], full_dst[:, n0:n1],
                                                    start=False, stop=False, skip_group_check=True)
                        last.then_inc(full_used, 1)
                    for a in range(2):
                        last = nc.tensor.matmul(ps[0:R, a, 0:HALF], zeros[:, 0:R], zeros[:, 0:HALF],
                                                start=False, stop=True, skip_group_check=True)
                    last.then_inc(full_ps, 1)
                pe.wait_ge(full_added, 2 * NT)

            def aggregate(a, m):
                if a == 0 and m == 0:
                    pe.wait_ge(adj_ready, 1)
                for c in range(NT):
                    last = nc.tensor.matmul(ps[:, 4 * m + a, 0:HALF], xn[:, c, m * 128:(m + 1) * 128],
                                            A[:, c, BEFORE + a * HALF:BEFORE + (a + 1) * HALF],
                                            start=(c == 0), stop=(c == NT - 1))
                last.then_inc(agg_ps, 1)

            def linear(layer, w, src):
                for a in range(2):
                    pe.wait_ge(agg_ready, (a + 1) * KC)
                    if layer:
                        pe.wait_ge(bn_ready, a + 1)
                        pe.wait_ge(lin_ready, (a + 1) * KC)
                    for m in range(KC):
                        for k in range(KC):
                            last = nc.tensor.matmul(ps[:, 4 * m + a, 0:HALF], w[:, k, m * 128:(m + 1) * 128],
                                                    src[:, k, a * HALF:(a + 1) * HALF], start=(k == 0), stop=(k == KC - 1))
                        last.then_inc(lin_ps, 1)

            def mix_attention(t):
                for k in range(KC):
                    nc.tensor.matmul(ps[0:R, MIX[t], 0:C], yT[:, k, t * R:(t + 1) * R], wproj_sb[:, k, :],
                                     start=(k == 0), stop=False, skip_group_check=True)

            def mix_gin(t):
                for m in range(KC):
                    last = nc.tensor.matmul(ps[0:R, MIX[t], m * 128:(m + 1) * 128], gT[:, m, t * R:(t + 1) * R], ident,
                                            start=False, stop=(m == KC - 1), skip_group_check=True)
                last.then_inc(mix_ps, 1)

            aggregate(0, 0)
            weigh(H // 2 - 1, 1)
            for a, m in ((0, 1), (1, 0), (1, 1)):
                aggregate(a, m)
            pe.wait_ge(wsmall_in, 80)
            linear(0, gw1_sb, gT)
            pe.wait_ge(y_ready, H + 2)
            for t in range(NT):
                if t >= 2:
                    pe.wait_ge(yT_ready, t - 1)
                for m in range(KC):
                    last = nc.tensor.transpose(ps[:, 2 + t % 2, m * R:(m + 1) * R],
                                               y[:, t, m * 128:(m + 1) * 128], ident[0:R, 0:R])
                last.then_inc(yT_ps, 1)
            pe.wait_ge(yT_ready, NT)
            for t in range(2):
                mix_attention(t)
            linear(1, gw2_sb, uT)
            for t in range(2, 4):
                mix_attention(t)
            pe.wait_ge(lin_ready, 4 * KC)
            mix_attention(4)
            pe.wait_ge(bn_ready, 4)
            for t in range(NT):
                mix_gin(t)

            for u in range(NT + 1):
                if u < NT:
                    pe.wait_ge(x2n_ready, u + 1)
                    for m in range(KC):
                        last = nc.tensor.transpose(ps[:, u % 2, m * R:(m + 1) * R],
                                                   x2n[:, u, m * 128:(m + 1) * 128], ident[0:R, 0:R])
                    last.then_inc(x2T_ps, 1)
                if u >= 1:
                    t = u - 1
                    pe.wait_ge(x2T_ready, t + 1)
                    for k in range(KC):
                        last = nc.tensor.matmul(ps[0:R, 7, t * NX:(t + 1) * NX], x2T[:, k, t * R:(t + 1) * R],
                                                gatew_sb[:, k, :], start=(k == 0), stop=(k == KC - 1))
            last.then_inc(gate_ps, 1)
            pe.wait_ge(sel_ready, 1)
            nc.tensor.matmul(ps[0:R, 5, 0:NT * NX], tri[0:R, 0:R], sel[:, :, :].rearrange("p t e -> p (t e)"),
                             start=True, stop=False, skip_group_check=True)
            for t in range(NT):
                last = nc.tensor.matmul(ps[0:R, 5, (t + 1) * NX:(NT + 1) * NX].rearrange("p (t e) -> p t e", e=NX),
                                        ones16[0:R, 0:R], sel[:, t:t + 1, :].to_broadcast([R, NT - t, NX]),
                                        start=False, stop=(t == NT - 1), skip_group_check=True)
            last.then_inc(rank_ps, 1)
            pe.wait_ge(cw_ready, 1)
            for t in range(NT):
                o = ps[0:NX, 7, t * R:(t + 1) * R] if t < 4 else ps[0:NX, 6, 0:R]
                last = nc.tensor.transpose(o, cw[:, t, :], ident[0:R, 0:R])
            last.then_inc(cwT_ps, 1)

            def expert_biases(t):
                bank, at = BIAS[t]
                nc.tensor.matmul(ps[0:R, bank, at:at + C], cwT[:, t * R:(t + 1) * R],
                                 fb2_sb[:, :], start=True, stop=True).then_inc(bias_ps, 1)

            pe.wait_ge(cwT_ready, 2)
            for t in range(3):
                expert_biases(t)
            pe.wait_ge(place_ready, 1)
            for r in range(2 * NT):
                last = nc.tensor.matmul(ps[:, 0, 0:XTILES], oh_place[:, r, :], row_tile[:, r, :],
                                        start=(r == 0), stop=(r == 2 * NT - 1))
            last.then_inc(slots_ps, 1)
            for t in range(3, NT):
                expert_biases(t)

            pe.wait_ge(dest_ready, 1)
            n_tiles = pe.value_load(meta_i[0:1, XTILES:XTILES + 1], min_val=XTILES_MIN, max_val=XTILES)
            pe.wait_ge(fw_in, 32 * NX)

            def expert_of(g):
                return pe.value_load(meta_i[0:1, bass.ds(g, 1)], min_val=0, max_val=NX - 1)

            def turn_x(g):
                if g is not None:
                    pe.wait_ge(x_copied, g)
                for k in range(KC):
                    last = nc.tensor.transpose(ps[:, 2, k * 128:(k + 1) * 128], x_rows[:, k * 128:(k + 1) * 128], ident)
                last.then_inc(x_turned, 1)

            def up(g, e):
                pe.wait_ge(xT_copied, g + 1)
                for k in range(KC):
                    last = nc.tensor.matmul(ps[:, 0, 0:HID], xT_t[:, k, :],
                                            arena[:, bass.ds(e * EXPERT + k * HID, HID)],
                                            start=(k == 0), stop=(k == KC - 1))
                last.then_inc(up_ps, 1)

            def turn_h(g):
                pe.wait_ge(up_copied, g + 1)
                for m in range(MC):
                    last = nc.tensor.transpose(ps[:, 1, m * 128:(m + 1) * 128], h_rows[:, m * 128:(m + 1) * 128], ident)
                last.then_inc(h_turned, 1)

            def down(g, e):
                pe.wait_ge(y_copied, g + 1)
                pe.wait_ge(gelu_ready, (g + 1) * MC)
                for m in range(MC):
                    last = nc.tensor.matmul(ps[:, 3, 0:C], hT_t[:, m, :],
                                            arena[:, bass.ds(e * EXPERT + (KC * HID + m * C), C)],
                                            start=(m == 0), stop=(m == MC - 1))
                last.then_inc(down_ps, 1)

            pe.wait_ge(tile_in[0], 16)
            turn_x(None)
            up(0, expert_of(0))
            turn_x(1)
            with pe.Fori(0, n_tiles - 1) as g:
                turn_h(g)
                up(g + 1, expert_of(g + 1))
                turn_x(g + 2)
                down(g, expert_of(g))
            turn_h(n_tiles - 1)
            down(n_tiles - 1, expert_of(n_tiles - 1))


def kernel(**inputs):
    import numpy as np
    import concourse.bacc as bacc
    from concourse.bass_utils import run_bass_kernel_spmd

    a = {k: np.asarray(v) for k, v in inputs.items()}
    f32 = np.float32

    def edge_tiles(v, fill):
        pad = np.full(TILES * 128, fill, v.dtype)
        pad[:E] = v
        return np.ascontiguousarray(pad.reshape(TILES, 128).T)

    cst = np.zeros((128, CSTS), f32)
    cst[:, CST_ID:CST_ID + 128] = np.eye(128, dtype=f32)
    cst[:, CST_IOTA:CST_IOTA + 128] = np.arange(128, dtype=f32)
    first = [STEP * (t // TILES_REG) + TILE_OFF[t % TILES_REG] for t in range(TILES)]
    cst[:, CST_KEY:CST_KEY + TILES] = np.array([NT * (BEFORE - f) for f in first], f32)
    cst[:, CST_RANK:CST_RANK + NX] = np.arange(NX, 0, -1, dtype=f32)
    cst[:, CST_DST:CST_DST + N] = np.arange(N, dtype=f32)
    cst[:, CST_TRI:CST_TRI + 128] = np.triu(np.ones((128, 128), f32), 1)
    cst[:, CST_THR:CST_THR + NT] = 128 * np.arange(NT, dtype=f32)
    cst[:, CST_LT:CST_LT + NX * NX] = np.tril(np.ones((NX, NX), f32), -1).reshape(-1)
    cst[:, CST_G:CST_G + XTILES] = np.arange(XTILES, dtype=f32)
    p = np.arange(128, dtype=f32)[:, None]
    cst[:, CST_ROW:CST_ROW + 2 * NT] = 1 + 2 * (p + R * np.arange(2 * NT)[None] % (R * NT)) + np.arange(2 * NT)[None] // NT
    cst[:, CST_EMPTY:CST_EMPTY + XTILES] = 2 * N + 1 + p + 128 * np.arange(XTILES)[None]

    def by_partition(v):
        return v.reshape(-1, 128).T

    cols = np.concatenate([by_partition(a["L0_gnn_" + k]) for k in ("b1", "g1", "be1", "b2", "g2", "be2")]
                          + [by_partition(a["L0_ffn_b1"].reshape(-1))], axis=1)
    rows = np.concatenate([a["L0_mix_bqkv"], a["L0_mix_bproj"], a["L0_ffn_gate_b"],
                           a["L0_mix_temperature"].reshape(-1), a["L0_gnn_eps"]])
    arrays = {
        "x": a["x"], "esrc": edge_tiles(a["src"], 0), "edst": edge_tiles(a["dst"], N - 1),
        "ew": edge_tiles(a["edge_weight"], 0), "cst": cst, "cols": cols, "rows": rows,
        "wqkvT": a["L0_mix_Wqkv"].T, "wprojT": a["L0_mix_Wproj"].T, "gw1": a["L0_gnn_W1"], "gw2": a["L0_gnn_W2"],
        "gatew": a["L0_ffn_gate_w"], "fw1": a["L0_ffn_W1"], "fw2": a["L0_ffn_W2"], "fb2": a["L0_ffn_b2"],
    }
    arrays = {k + "_dram": np.ascontiguousarray(v) for k, v in arrays.items()}
    nc = bacc.Bacc("TRN2", target_bir_lowering=False, num_devices=1)
    args = [nc.dram_tensor(k, v.shape, mybir.dt.from_np(v.dtype), kind="ExternalInput").ap() for k, v in arrays.items()]
    out = nc.dram_tensor("out_dram", (N, C), F32, kind="ExternalOutput").ap()
    graph_layer(nc, *args, out)
    r = run_bass_kernel_spmd(nc, [arrays], core_ids=[0])
    return r.results[0]["out_dram"]
```
